# Optimizing a Trainium2 kernel written in Bass

```python
import numpy as np
import jax
import jax.numpy as jnp

def _softmax(x, axis=-1):
    return jax.nn.softmax(x, axis=axis)

def _gelu(x):
    return jax.nn.gelu(x, approximate=True)

def _silu(x):
    return jax.nn.silu(x)

def _sigmoid(x):
    return jax.nn.sigmoid(x)

def _layernorm(x, axis=-1, eps=1e-05):
    m = jnp.mean(x, axis=axis, keepdims=True)
    v = jnp.var(x, axis=axis, keepdims=True)
    return (x - m) / jnp.sqrt(v + eps)

def _scatter_add(tgt, idx, src, axis=0):
    return tgt.at[idx].add(src)

def _segment_sum(src, seg, n):
    return jax.ops.segment_sum(src, seg, n)
kernel_name = 'mk_gnn_resnorm_d2_gnn_r32_22a61f'

def setup_inputs(seed: int=0):
    np.random.seed(seed)
    _w = jnp.asarray

    def _rec_inputs():
        import jax
        import jax.numpy as jnp
        _gk = jax.random.key(seed)
        x = -0.000202 + 1 * jax.random.normal(jax.random.fold_in(_gk, 1), (3125, 128), jnp.float32)
        _s = jax.random.randint(jax.random.fold_in(_gk, 2), (25000,), 0, 3125, jnp.int32)
        _d = jax.random.randint(jax.random.fold_in(_gk, 3), (25000,), 0, 3125, jnp.int32)
        _loop = jnp.arange(3125, dtype=jnp.int32)
        src = jnp.concatenate([_s, _d, _loop])
        dst = jnp.concatenate([_d, _s, _loop])
        _o = jnp.argsort(dst, stable=True)
        src = src[_o]
        dst = dst[_o]
        edge_type_32 = jax.random.randint(jax.random.fold_in(_gk, 13), (53125,), 0, 32, jnp.int32)
        edge_weight1 = jax.random.uniform(jax.random.fold_in(_gk, 14), (53125, 1), jnp.float32, 0.0, 0.999998)
        return (x, src, dst, edge_type_32, edge_weight1)
    x, src, dst, edge_type_32, edge_weight1 = _rec_inputs()

    def _L0_gnn_setup():
        import jax, jax.numpy as jnp
        import numpy as np
        N, E, D, F, R, B = (50000, 50000, 128, 128, 32, 8)
        key = jax.random.key(seed)
        ks = jax.random.split(key, 9)
        h = jax.random.normal(ks[0], (N, D), dtype=jnp.float32)
        src = jax.random.randint(ks[1], (E,), 0, N, dtype=jnp.int32)
        dst = jax.random.randint(ks[2], (E,), 0, N, dtype=jnp.int32)
        etype = jax.random.randint(ks[3], (E,), 0, R, dtype=jnp.int32)
        norm = jax.random.uniform(ks[4], (E, 1), dtype=jnp.float32)
        weight = jax.random.normal(ks[5], (B, D, F), dtype=jnp.float32) * (2.0 / (D + F)) ** 0.5
        w_comp = jax.random.normal(ks[6], (R, B), dtype=jnp.float32) * (2.0 / (R + B)) ** 0.5
        loop_weight = jax.random.normal(ks[7], (D, F), dtype=jnp.float32) * (2.0 / (D + F)) ** 0.5
        h_bias = jnp.zeros((F,), dtype=jnp.float32)
        return {'h': h, 'src': src, 'dst': dst, 'etype': etype, 'norm': norm, 'weight': weight, 'w_comp': w_comp, 'loop_weight': loop_weight, 'h_bias': h_bias}
    _L0_gnn_all = _L0_gnn_setup()
    _L0_gnn_in = {k: v for k, v in _L0_gnn_all.items() if k in ('weight', 'w_comp', 'loop_weight', 'h_bias')}
    del _L0_gnn_all

    def _L1_gnn_setup():
        import jax, jax.numpy as jnp
        import numpy as np
        N = 3125
        E = 18750
        DIN = 128
        DOUT = 128
        key = jax.random.key(seed)
        k1, k2, k3 = jax.random.split(key, 3)
        x = jax.random.normal(k1, (N, DIN), dtype=jnp.float32)
        edge_index = jax.random.randint(k2, (2, E), 0, N, dtype=jnp.int64)
        W = jax.random.normal(k3, (DIN, DOUT), dtype=jnp.float32) * (1.0 / np.sqrt(DIN))
        b = jnp.zeros((DOUT,), dtype=jnp.float32)
        return {'x': x, 'edge_index': edge_index, 'W': W, 'b': b}
    _L1_gnn_all = _L1_gnn_setup()
    _L1_gnn_in = {k: v for k, v in _L1_gnn_all.items() if k in ('W', 'b')}
    del _L1_gnn_all
    return {'x': x, 'src': src, 'dst': dst, 'edge_type_32': edge_type_32, 'edge_weight1': edge_weight1, 'L0_gnn_weight': _L0_gnn_in['weight'], 'L0_gnn_w_comp': _L0_gnn_in['w_comp'], 'L0_gnn_loop_weight': _L0_gnn_in['loop_weight'], 'L0_gnn_h_bias': _L0_gnn_in['h_bias'], 'L1_gnn_W': _L1_gnn_in['W'], 'L1_gnn_b': _L1_gnn_in['b']}

def reference(x, src, dst, edge_type_32, edge_weight1, L0_gnn_weight, L0_gnn_w_comp, L0_gnn_loop_weight, L0_gnn_h_bias, L1_gnn_W, L1_gnn_b):
    import jax
    import jax.numpy as jnp

    def _L0_gnn_ref(h, src, dst, etype, norm, weight, w_comp, loop_weight, h_bias):
        import jax, jax.numpy as jnp
        import numpy as np
        N, E, D, F, R, B = (50000, 50000, 128, 128, 32, 8)
        n_nodes, d_in = h.shape
        n_rels = w_comp.shape[0]
        W_rel = jnp.einsum('rb,bdf->rdf', w_comp, weight)
        seg = etype * n_nodes + dst
        agg = jax.ops.segment_sum(h[src] * norm, seg, num_segments=n_rels * n_nodes)
        agg = agg.reshape(n_rels, n_nodes, d_in)
        node_repr = jnp.einsum('rnd,rdf->nf', agg, W_rel)
        node_repr = node_repr + h_bias + h @ loop_weight
        return jax.nn.relu(node_repr)

    def _L1_gnn_ref(x, edge_index, W, b):
        import jax, jax.numpy as jnp
        import numpy as np
        N = 3125
        E = 18750
        DIN = 128
        DOUT = 128
        n = x.shape[0]
        loop = jnp.arange(n, dtype=edge_index.dtype)
        src = jnp.concatenate([edge_index[0], loop])
        dst = jnp.concatenate([edge_index[1], loop])
        xw = x @ W
        deg = jax.ops.segment_sum(jnp.ones_like(dst, dtype=xw.dtype), dst, num_segments=n)
        dinv = jnp.where(deg > 0, jax.lax.rsqrt(deg), 0.0)
        norm = dinv[src] * dinv[dst]
        msg = xw[src] * norm[:, None]
        out = jax.ops.segment_sum(msg, dst, num_segments=n)
        return out + b
    edge_index = jnp.stack([src, dst])
    x = _layernorm(x + _L0_gnn_ref(x, src, dst, edge_type_32, edge_weight1, L0_gnn_weight, L0_gnn_w_comp, L0_gnn_loop_weight, L0_gnn_h_bias), axis=-1)
    x = _layernorm(x + _L1_gnn_ref(x, edge_index, L1_gnn_W, L1_gnn_b), axis=-1)
    return x

_drawn_inputs = setup_inputs


def setup_inputs(seed=0):
    import zlib

    import numpy as np

    out = dict(_drawn_inputs(seed))
    spreads = {'L0_gnn_h_bias': (0.0, 0.1), 'L1_gnn_b': (0.0, 0.1)}
    factors = {}
    for name, (base, spread) in spreads.items():
        noise = np.random.default_rng([zlib.crc32(name.encode()), seed]).standard_normal(out[name].shape)
        drawn = base * np.exp(spread * noise) if base else spread * noise
        out[name] = jnp.asarray(drawn.astype(out[name].dtype))
    for name, factor in factors.items():
        out[name] = (out[name] * factor).astype(out[name].dtype)
    return out
```

```python
from contextlib import ExitStack

import concourse.bass as bass
import concourse.mybir as mybir

F32, F16, I32, U8 = mybir.dt.float32, mybir.dt.float16, mybir.dt.int32, mybir.dt.uint8
ALU = mybir.AluOpType
ACT = mybir.ActivationFunctionType
AX = mybir.AxisListType

P = 128
NODES, FEAT, EDGES, RELS, BASES = 3125, 128, 53125, 32, 8
CHUNKS = -(-EDGES // P)
GROUP = 8
STEP = 2 * GROUP
STEPS = CHUNKS // STEP
WIN = 12
TILES = -(-NODES // P)
LAST = NODES - (TILES - 1) * P
NPAD = 3136
KEYS = TILES * WIN
ROWS = TILES + 1
LEAD = STEP
LAG = 2
EPS = 1e-5
ACT_ROWS = 10
LOSCALE = 2048.0
Q = P // RELS
BLOCK = 512


def gnn_kernel(nc, x, src_idx, src_t, dst_t, src_rows, dst_rows, starts, types, type_rows, norm_t, weight, w_comp, loop_w,
               bias0, w1, bias1, out):
    ctx = ExitStack()
    with ctx:
        def sb(name, shape, dt):
            return ctx.enter_context(nc.sbuf_tensor(name, shape, dt))

        def sem(name):
            return ctx.enter_context(nc.semaphore(name))

        cnt16 = sb("cnt16", [P, 2, TILES, BLOCK], F16)
        arena, used = cnt16[:].rearrange("p a b c -> p (a b c)"), [0]

        def carve(dims, dt, size):
            n = 1
            for d in dims:
                n *= d
            at, used[0] = used[0], used[0] + -(-n * size // 64) * 32
            assert used[0] <= 2 * TILES * BLOCK
            flat = arena[:, at:at + n * size // 2]
            flat = flat if dt == F16 else flat.bitcast(dt)
            names = "abcd"[:len(dims)]
            return flat.rearrange(f"p ({' '.join(names)}) -> p {' '.join(names)}", **dict(zip(names[1:], dims[1:])))

        x_nm = sb("x_nm", [P, TILES, FEAT], F32)
        norm = carve([CHUNKS + STEP], F32, 4)
        start_i = sb("start_i", [1, LEAD + CHUNKS], I32)
        wt = sb("wt", [FEAT, BASES, FEAT], F32)
        wcomp_bd = sb("wcomp_bd", [P, (2 * Q - 1) * Q * BASES], F32)
        loop_sb = sb("loop_sb", [FEAT, FEAT], F32)
        w1_sb = sb("w1_sb", [FEAT, FEAT], F32)
        bias0_col = sb("bias0_col", [FEAT, 1], F32)
        bias1_b = sb("bias1_b", [P, FEAT], F32)
        ident = sb("ident", [P, P], F32)
        iota_lo = sb("iota_lo", [P, P], F16)
        iota_key = sb("iota_key", [P, KEYS], F16)
        rel_id = sb("rel_id", [P, 1], F32)
        lane_i = sb("lane_i", [P, 1], I32)
        rel_id_i = sb("rel_id_i", [P, 1], I32)
        ones16 = sb("ones16", [P, 1], F16)
        eps_col = sb("eps_col", [P, 1], F32)
        neg_lo = sb("neg_lo", [P, CHUNKS + STEP], F32)
        rel = carve([CHUNKS + STEP], F32, 4)
        key = carve([CHUNKS], F32, 4)
        idx = sb("idx", [P, 2, GROUP], I32)
        rows = carve([STEP, FEAT], F32, 4)
        typ = carve([Q, P], I32, 4)
        typ_oh = carve([Q, P], F32, 4)
        coef_raw = carve([STEP * BASES], F32, 4)
        coef = carve([STEP, BASES], F32, 4)
        scat = carve([2, GROUP, BASES, WIN], F32, 4)
        key_oh = carve([2, GROUP, KEYS + WIN], F16, 2)
        win_oh = key_oh[:, :, :, KEYS:]
        lo_abs = carve([GROUP, P], F16, 2)
        lo_oh = carve([2, GROUP, P], F16, 2)
        g_sb = carve([2, BASES, GROUP * WIN], F32, 4)
        count = sb("count", [P, ROWS, NPAD], U8)
        acc = sb("acc", [FEAT, NPAD], F32)
        xt = sb("xt", [FEAT, TILES * P], F32)
        e_src, e_dst, e_to = sb("e_src", [P, 1], I32), sb("e_dst", [P, 1], I32), sb("e_to", [P, 1], I32)
        e_dstf, e_flag, e_far = sb("e_dstf", [P, 1], F32), sb("e_flag", [P, 1], F32), sb("e_far", [P, 1], F32)
        e_coef = sb("e_coef", [P, BASES], F32)
        lane, spare, least = sb("lane", [P, 1], F32), sb("spare", [P, 1], F32), sb("least", [P, 1], F32)
        bad, ones32, flag = sb("bad", [P, 1], F32), sb("ones32", [P, 1], F32), sb("flag", [1, 1], I32)
        deg = sb("deg", [P, TILES], F32)
        dinv = sb("dinv", [P, TILES], F32)
        h_nm = sb("h_nm", [P, TILES, FEAT], F32)
        early = h_nm[:].rearrange("p t f -> p (t f)")[:, 0:4 * CHUNKS].bitcast(I32).rearrange("p (a k) -> p a k", a=4)
        src_i, dst_i, start_b, work_i = (early[:, n] for n in range(4))
        z_hi = sb("z_hi", [P, TILES, FEAT], F16)
        deg_part = z_hi[:].rearrange("p t f -> p (t f)")[:, 0:NPAD]
        z_lo = sb("z_lo", [P, TILES, FEAT], F16)
        stats = sb("stats", [P, TILES, 6], F32)
        mv = sb("mv", [P, TILES, 2], F32)
        rstd = sb("rstd", [P, TILES], F32)
        sdev = sb("sdev", [P, TILES], F32)
        scale_z = sb("scale_z", [P, TILES], F32)
        z_f = xt[:].rearrange("p (t f) -> p t f", f=FEAT)

        bank = [ctx.enter_context(nc.psum_tensor(f"bank{n}", [P, 512], F32)) for n in range(8)]
        cnt_ps, g_ps, z_ps = bank[0:4], bank[4:6], bank[6:8]
        coef_ps = g_ps[1][:, 4 * BASES * WIN:]

        def s16(n):
            return [sem(f"{n}{k}") for k in range(STEP)]
        gathered = s16("gathered")
        slot_free = sem("slot_free")
        idx_loaded = [sem("idx_loaded0"), sem("idx_loaded1")]
        ld_edges, ld_x, ld_w = sem("ld_edges"), sem("ld_x"), sem("ld_w")
        win_ready = sem("win_ready")
        typ_loaded, typ_done = sem("typ_loaded"), sem("typ_done")
        coef_ready, coef_copied, coef_taken = sem("coef_ready"), sem("coef_copied"), sem("coef_taken")
        iotas, wbd_zero, tail_zero = sem("iotas"), sem("wbd_zero"), sem("tail_zero")
        dve, counts_added, rows_added = sem("dve"), sem("counts_added"), sem("rows_added")
        nums_ready = sem("nums_ready")
        scat_ready, key_ready, lo_ready, lo_step = sem("scat_ready"), sem("key_ready"), sem("lo_ready"), sem("lo_step")
        g_ready, g_taken, cnt_ready = sem("g_ready"), sem("g_taken"), sem("cnt_ready")
        z_ready = sem("z_ready")
        xt_ready, xt_taken, init_ready, init_taken = sem("xt_ready"), sem("xt_taken"), sem("init_ready"), sem("init_taken")
        deg_ready, degt_ready, t_ready, t_taken = sem("deg_ready"), sem("degt_ready"), sem("t_ready"), sem("t_taken")
        deg_taken, var_ready, sd_ready, tail = sem("deg_taken"), sem("var_ready"), sem("sd_ready"), sem("tail")
        zf_ready, zhi_ready, zd_ready, zlo_ready = sem("zf_ready"), sem("zhi_ready"), sem("zd_ready"), sem("zlo_ready")
        cv_dve, cv_act = sem("cv_dve"), sem("cv_act")
        agg_ready, agg_copied, agg_done = sem("agg_ready"), sem("agg_copied"), sem("agg_done")
        fin_ready, fin_taken, var1, sd1, out_ready, stored = sem("fin_ready"), sem("fin_taken"), sem("var1"), sem("sd1"), sem("out_ready"), sem("stored")

        flag_ready, bad_ready, bad_summed = sem("flag_ready"), sem("bad_ready"), sem("bad_summed")
        sums_ready = sem("sums_ready")
        events = ("loaded", "gathered", "turned", "xt", "types", "products", "message", "to", "summed", "total",
                  "added", "chunk_free", "cleared", "z", "dve", "back", "back_turned", "back_added", "back_taken")
        general = [{e: sem(f"general{n}_{e}") for e in events} for n in range(2)]
        general[0]["clears"], general[1]["clears"] = TILES + 1, 2 * TILES + 1
        sums = [nc.dram_tensor(f"sums{n}", (NODES + P, FEAT + 1 - n), F32, kind="Internal").ap() for n in range(2)]
        z_dram = nc.dram_tensor("z_dram", (NODES, FEAT), F32, kind="Internal").ap()
        e_rows, e_xt, same, earlier, before = (rows[:, n] for n in range(5))
        dst_row, e_typ, e_typ_oh = rows[:, 5].bitcast(I32), rows[0:RELS, 6].bitcast(I32), rows[0:RELS, 7]
        pair = rows[:].rearrange("p (a b) f -> p a (b f)", b=2)
        message, total = pair[:, 4], pair[:, 5]

        full = TILES - 1
        tiles = [(t, P if t < full else LAST) for t in range(TILES)]
        quads = [tiles[a:a + 4] for a in range(0, TILES, 4)]
        blocks = [(a, min(BLOCK, NODES - a)) for a in range(0, NODES, BLOCK)]

        block = ctx.enter_context(nc.Block())

        def is_narrow(eng):
            eng.wait_ge(flag_ready, 1)
            return eng.value_load(flag[0:1, 0:1], min_val=0, max_val=1) == 0

        def general_sync(sp, layer):
            g = general[layer]
            if layer == 0:
                source = g_sb[:, 0].rearrange("p b n -> p (b n)")[:, 0:FEAT + 1]
                sp.wait_ge(g_taken, 4)
                for j in range(STEP):
                    sp.wait_ge(gathered[j], 16)
                for t in range(TILES + 1):
                    r = min(P, NODES + P - t * P)
                    sp.dma_start(sums[0][t * P:t * P + r, :], source[0:r, :]).then_inc(g["cleared"], 16)
            else:
                sp.wait_ge(g["z"], 1)
                for t, r in tiles:
                    sp.dma_start(sums[1][t * P:t * P + r, :], z_f[0:r, t, :]).then_inc(g["cleared"], 16)
                    sp.dma_start(z_dram[t * P:t * P + r, :], z_f[0:r, t, :]).then_inc(g["cleared"], 16)
                sp.dma_start(sums[1][NODES:NODES + P, :], z_f[:, 0, :]).then_inc(g["cleared"], 16)
            sp.wait_ge(g["cleared"], 16 * g["clears"])
            sp.sem_inc(g["chunk_free"], 1)
            with sp.Fori(0, CHUNKS) as k:
                sp.wait_ge(g["chunk_free"], k + 1)
                sp.dma_start(e_src[:], src_rows[bass.ds(k, 1), :].rearrange("o p -> p o")).then_inc(g["loaded"], 16)
                sp.dma_start(e_dst[:], dst_rows[bass.ds(k, 1), :].rearrange("o p -> p o")).then_inc(g["loaded"], 16)
                sp.dma_start(dst_row, dst_rows[bass.ds(k, 1), :].broadcast_to([P, P])).then_inc(g["loaded"], 16)
                sp.dma_start(e_typ, type_rows[bass.ds(k, 1), :].broadcast_to([RELS, P])).then_inc(g["loaded"], 16)
            sp.wait_ge(g["chunk_free"], CHUNKS + 1)
            width = FEAT + 1 - layer
            for t, r in tiles:
                if t:
                    sp.wait_ge(g["back_taken"], t)
                sp.dma_start(total[0:r, 0:width], sums[layer][t * P:t * P + r, :]).then_inc(g["back"], 16)

        def general_gpsimd(pool, layer):
            g = general[layer]
            table, rows_in = (x, e_rows) if layer == 0 else (z_dram, message[:, 0:FEAT])
            width = FEAT + 1 - layer
            with pool.Fori(0, CHUNKS) as k:
                pool.wait_ge(g["loaded"], 64 * k + 64)
                pool.sem_inc(slot_free, 1)
                pool.indirect_dma_start(rows_in, None, table[:, :],
                                        bass.IndirectOffsetOnAxis(ap=e_src[:], axis=0)).then_inc(g["gathered"], 16)
                pool.wait_ge(g["total"], k + 1)
                pool.sem_inc(slot_free, 1)
                pool.indirect_dma_start(sums[layer][:, :], bass.IndirectOffsetOnAxis(ap=e_to[:], axis=0),
                                        total[:, 0:width], None, compute_op=ALU.add).then_inc(g["added"], 16)
                pool.wait_ge(g["added"], 16 * k + 16)
                pool.sem_inc(g["chunk_free"], 1)

        def general_scalar(act, layer):
            g = general[layer]
            if layer == 0:
                with act.Fori(0, CHUNKS) as k:
                    act.wait_ge(g["turned"], k + 1)
                    nc.scalar.copy(e_xt, bank[0][:, 0:P]).then_inc(g["xt"], 1)

        def general_vector(v, layer):
            g = general[layer]
            width = FEAT + 1 - layer
            if layer == 1:
                for t, _ in tiles:
                    ins = nc.vector.tensor_scalar(z_f[:, t, :], x_nm[:, t, :], mv[:, t, 0:1], scale_z[:, t:t + 1],
                                                  ALU.subtract, ALU.mult)
                ins.then_inc(g["z"], 1)
            else:
                for j in range(STEP):
                    v.wait_ge(gathered[j], 16)
            nc.vector.tensor_scalar(before, iota_lo[:], lane[:], None, ALU.is_lt).then_inc(g["dve"], 1)
            with v.Fori(0, CHUNKS) as k:
                n = [0]

                def link(ins):
                    n[0] += 1
                    ins.then_inc(g["dve"], 1)
                    v.wait_ge(g["dve"], steps * k + n[0] + 1)
                steps = 6 + (1 + BASES if layer == 0 else 0)
                v.wait_ge(g["loaded"], 64 * k + 64)
                link(nc.vector.tensor_copy(e_dstf[:], e_dst[:]))
                link(nc.vector.tensor_scalar(same, dst_row, e_dstf[:], None, ALU.is_equal))
                link(nc.vector.tensor_tensor(earlier, same, before, ALU.mult))
                link(nc.vector.tensor_reduce(e_flag[:], earlier, AX.X, ALU.max))
                link(nc.vector.scalar_tensor_tensor(e_flag[:], e_dstf[:], 0.0, e_flag[:], ALU.is_lt, ALU.max))
                link(nc.vector.tensor_scalar(e_far[:], e_dstf[:], -1.0, spare[:], ALU.mult, ALU.add))
                nc.vector.scalar_tensor_tensor(e_to[:], e_far[:], e_flag[:], e_dstf[:], ALU.mult, ALU.add).then_inc(g["to"], 1)
                if layer == 0:
                    nc.vector.tensor_scalar(e_typ_oh, e_typ, rel_id[0:RELS, :], None, ALU.is_equal).then_inc(g["types"], 1)
                    v.wait_ge(g["products"], k + 1)
                    link(nc.vector.tensor_scalar(e_coef[:], bank[3][:, 0:BASES], norm[:, bass.ds(k, 1)], None, ALU.mult))
                    for b in range(BASES):
                        product = bank[1 + b // 4][:, (b % 4) * FEAT:(b % 4 + 1) * FEAT]
                        if b == 0:
                            link(nc.vector.tensor_scalar(message[:, 0:FEAT], product, e_coef[:, 0:1], None, ALU.mult))
                        else:
                            link(nc.vector.scalar_tensor_tensor(message[:, 0:FEAT], product, e_coef[:, b:b + 1],
                                                                message[:, 0:FEAT], ALU.mult, ALU.add))
                    nc.vector.tensor_scalar(message[:, FEAT:FEAT + 1], e_dstf[:], 0.0, None,
                                            ALU.is_ge).then_inc(g["message"], 1)
                assert n[0] == steps
                v.wait_ge(g["summed"], k + 1)
                v.wait_ge(g["to"], k + 1)
                nc.vector.tensor_copy(total[:, 0:width], bank[4][:, 0:width]).then_inc(g["total"], 1)
            for t, r in tiles:
                v.wait_ge(g["back_turned"], t + 1)
                to, ps = acc[:, t * P:t * P + r], bank[t % 2][:, 0:r]
                if layer == 0:
                    nc.vector.tensor_tensor(to, to, ps, ALU.add).then_inc(g["back_added"], 1)
                    v.wait_ge(g["back"], 16 * t + 16)
                    nc.vector.tensor_scalar(deg[0:r, t:t + 1], total[0:r, FEAT:FEAT + 1], 1.0, None,
                                            ALU.add).then_inc(g["back_taken"], 1)
                else:
                    nc.vector.tensor_copy(to, ps).then_inc(g["back_added"], 1)
                    nc.vector.engine_nop().then_inc(g["back_taken"], 1)
            v.wait_ge(g["back_added"], TILES)

        def general_tensor(pe, layer):
            g = general[layer]
            width = FEAT + 1 - layer
            with pe.Fori(0, CHUNKS) as k:
                pe.wait_ge(g["gathered"], 16 * k + 16)
                if layer == 0:
                    nc.tensor.transpose(bank[0][:, 0:P], e_rows, ident[:]).then_inc(g["turned"], 1)
                    pe.wait_ge(g["types"], k + 1)
                    at = (Q - 1) * Q * BASES
                    nc.tensor.matmul(bank[3][:, 0:BASES], e_typ_oh, wcomp_bd[0:RELS, at:at + BASES], start=True, stop=True)
                    pe.wait_ge(g["xt"], k + 1)
                    for half in range(2):
                        last = nc.tensor.matmul(bank[1 + half][:], e_xt,
                                                wt[:, 4 * half:4 * half + 4, :].rearrange("p b f -> p (b f)"),
                                                start=True, stop=True)
                    last.then_inc(g["products"], 1)
                    pe.wait_ge(g["message"], k + 1)
                else:
                    pe.wait_ge(g["to"], k + 1)
                nc.tensor.matmul(bank[4][:, 0:width], same, message[:, 0:width], start=True, stop=True).then_inc(g["summed"], 1)
            for t, r in tiles:
                pe.wait_ge(g["back"], 16 * t + 16)
                if t >= 2:
                    pe.wait_ge(g["back_added"], t - 1)
                nc.tensor.transpose(bank[t % 2][:, 0:r], total[0:r, 0:FEAT], ident[0:r, 0:r]).then_inc(g["back_turned"], 1)

        @block.sync
        def _(sp):
            def load_idx(i, h):
                sp.dma_start(idx[:, h, :], src_idx[bass.ds(i, 1), h].rearrange("o p k -> (o p) k")).then_inc(idx_loaded[h], 16)

            def load_types(i):
                for q in range(Q):
                    sp.dma_start(typ[RELS * q:RELS * (q + 1), :, :].rearrange("p a b -> p (a b)"),
                                 types[bass.ds(i, 1), q].rearrange("o u n -> (o u) n").broadcast_to([RELS, Q * P])).then_inc(typ_loaded, 16)
            for h in range(2):
                sp.dma_start(idx[:, h, :], src_idx[0, h]).then_inc(idx_loaded[h], 16)
            sp.dma_start(src_i, src_t).then_inc(ld_edges, 16)
            sp.dma_start(dst_i, dst_t).then_inc(ld_edges, 16)
            sp.dma_start(start_b, starts[:, LEAD:LEAD + CHUNKS].broadcast_to([P, CHUNKS])).then_inc(ld_edges, 16)
            sp.dma_start(start_i[:], starts).then_inc(ld_edges, 16)
            sp.dma_start(norm[:, 0:CHUNKS], norm_t).then_inc(ld_edges, 16)
            load_types(0)
            sp.wait_ge(tail_zero, 1)
            sp.dma_start(x_nm[:, 0:full, :], x[0:full * P, :].rearrange("(t p) f -> p t f", p=P)).then_inc(ld_x, 16)
            sp.dma_start(x_nm[0:LAST, full, :], x[full * P:NODES, :]).then_inc(ld_x, 16)
            sp.dma_start(loop_sb[:], loop_w).then_inc(ld_x, 16)
            sp.dma_start(bias0_col[:], bias0.rearrange("(f o) -> f o", o=1)).then_inc(ld_x, 16)
            sp.wait_ge(wbd_zero, 1)
            for q in range(Q):
                sp.dma_start(wcomp_bd[RELS * q:RELS * (q + 1), (Q - 1) * Q * BASES + BASES * q:(Q - 1) * Q * BASES + BASES * (q + 1)], w_comp).then_inc(ld_w, 16)
            sp.dma_start(wt[:], weight.rearrange("b d f -> d b f")).then_inc(ld_w, 16)
            sp.dma_start(w1_sb[:], w1).then_inc(ld_w, 16)
            sp.dma_start(bias1_b[:], bias1.rearrange("(o f) -> o f", o=1).broadcast_to([P, FEAT])).then_inc(ld_w, 16)
            narrow = is_narrow(sp)
            with sp.If(narrow):
                with sp.Fori(0, STEPS) as i:
                    sp.wait_ge(typ_done, i + 1)
                    load_types(i + 1)
                    for h in range(2):
                        for j in range(GROUP * h, GROUP * h + GROUP):
                            sp.wait_ge(gathered[j], 16 * i + 16)
                        load_idx(i + 1, h)
            with sp.Else():
                general_sync(sp, 0)
                general_sync(sp, 1)
            for n, quad in enumerate(quads):
                sp.wait_ge(out_ready, n + 1)
                t0, rows_in = quad[0][0], sum(r for _, r in quad)
                if rows_in == len(quad) * P:
                    sp.dma_start(out[t0 * P:(t0 + len(quad)) * P, :].rearrange("(t p) f -> p t f", p=P),
                                 x_nm[:, t0:t0 + len(quad), :]).then_inc(stored, 16)
                else:
                    sp.dma_start(out[t0 * P:NODES, :], x_nm[0:rows_in, t0, :]).then_inc(stored, 16)
            sp.wait_ge(stored, 16 * len(quads))

        @block.gpsimd
        def _(pool):
            def gather(j):
                return pool.indirect_dma_start(
                    rows[:, j, :], None, x[:, :],
                    bass.IndirectOffsetOnAxis(ap=idx[:, j // GROUP, j % GROUP:j % GROUP + 1], axis=0)).then_inc(gathered[j], 16)

            for h in range(2):
                pool.wait_ge(idx_loaded[h], 16)
                for j in range(GROUP * h, GROUP * h + GROUP):
                    gather(j)
                if h == 0:
                    nc.gpsimd.iota(iota_lo[:], [[1, P]], base=0, channel_multiplier=0, allow_small_or_imprecise_dtypes=True)
                    nc.gpsimd.iota(lane_i[:], [[0, 1]], base=0, channel_multiplier=1)
                    nc.gpsimd.iota(iota_key[:], [[1, KEYS]], base=0, channel_multiplier=0, allow_small_or_imprecise_dtypes=True).then_inc(iotas, 1)
                    nc.gpsimd.memset(ident[:], 1.0).then_inc(iotas, 1)
                    pool.wait_ge(iotas, 2)
                    nc.gpsimd.affine_select(out=ident[:], in_=ident[:], compare_op=ALU.is_equal, fill=0.0, base=0,
                                            pattern=[[-1, P]], channel_multiplier=1).then_inc(iotas, 1)
            narrow = is_narrow(pool)
            with pool.If(narrow):
                with pool.Fori(1, STEPS) as i:
                    for h in range(2):
                        pool.wait_ge(idx_loaded[h], 16 * i + 16)
                        for j in range(GROUP * h, GROUP * h + GROUP):
                            pool.wait_ge(cnt_ready, STEP * i - STEP + j + 1 + LAG)
                            pool.sem_inc(slot_free, 1)
                            gather(j)
            with pool.Else():
                general_gpsimd(pool, 0)
                general_gpsimd(pool, 1)

        @block.scalar
        def _(act):
            def lo_half(nc, act, n):
                t0, k = quads[n][0][0], len(quads[n])
                act.wait_ge(zd_ready, n + 1)
                nc.scalar.activation(z_lo[:, t0:t0 + k], z_f[:, t0:t0 + k], ACT.Copy, scale=LOSCALE).then_inc(zlo_ready, 1)

            def deviation(nc, act, n):
                t0, k = quads[n][0][0], len(quads[n])
                act.wait_ge(var1, n + 1)
                nc.scalar.activation(sdev[:, t0:t0 + k], mv[:, t0:t0 + k, 1], ACT.Sqrt, bias=eps_col[:]).then_inc(sd1, 1)

            def one_hot_lo(g, h, n):
                if not isinstance(n, int):
                    act.wait_ge(lo_ready, n - 1)
                for j in range(GROUP):
                    last = nc.scalar.activation(lo_abs[:, j, :], iota_lo[:], ACT.Abs, bias=neg_lo[:, bass.ds(GROUP * g + j, 1)])
                last.then_inc(lo_step, 1)
                act.wait_ge(lo_step, n)
                nc.scalar.activation(lo_oh[:, h], lo_abs[:], ACT.Relu, bias=1.0, scale=-1.0).then_inc(lo_ready, 1)

            for n, quad in enumerate(quads):
                width = sum(r for _, r in quad)
                act.wait_ge(xt_ready, n + 1)
                nc.scalar.copy(xt[:, n * 512:n * 512 + width], bank[n % 2][:, 0:width]).then_inc(xt_taken, 1)
            act.wait_ge(ld_x, 64)
            for n, (a, width) in enumerate(blocks):
                act.wait_ge(init_ready, n + 1)
                nc.scalar.activation(acc[:, a:a + width], bank[2 + n % 2][:, 0:width], ACT.Identity,
                                     bias=bias0_col[:]).then_inc(init_taken, 1)
            narrow = is_narrow(act)
            with act.If(narrow):
                one_hot_lo(0, 0, 1)
                act.wait_ge(coef_ready, 1)
                nc.scalar.copy(coef_raw[:], coef_ps[:]).then_inc(coef_copied, 1)
                act.wait_ge(coef_copied, 1)
                with act.Fori(0, STEPS) as i:
                    for h in range(2):
                        g = 2 * i + h
                        act.wait_ge(cnt_ready, GROUP * g + LAG)
                        one_hot_lo(g + 1, 1 - h, g + 2)
                        act.wait_ge(z_ready, g + 1)
                        for q in range(2):
                            act.wait_ge(g_ready, 2 * g + q + 1)
                            if h == 0 and q == 1:
                                act.wait_ge(coef_taken, i + 1)
                                nc.scalar.copy(coef_raw[:], coef_ps[:]).then_inc(coef_copied, 1)
                            nc.scalar.copy(g_sb[:, h].rearrange("p b (c n) -> p c b n", n=WIN)[:, 4 * q:4 * q + 4],
                                           g_ps[q][:, 0:4 * BASES * WIN].rearrange("p (c b n) -> p c b n", b=BASES, n=WIN)
                                           ).then_inc(g_taken, 1)
                act.wait_ge(deg_ready, 1)
                nc.scalar.copy(cnt16[:, 0, :, :], count[:, 0:TILES, 0:BLOCK]).then_inc(cv_act, 1)
            with act.Else():
                general_scalar(act, 0)
            act.wait_ge(deg_taken, 1)
            nc.scalar.activation(dinv[:], deg[:], ACT.Sqrt).then_inc(sd_ready, 1)
            act.wait_ge(var_ready, 1)
            nc.scalar.activation(sdev[:], mv[:, :, 1], ACT.Sqrt, bias=eps_col[:]).then_inc(sd_ready, 1)
            with act.If(narrow):
                for n, quad in enumerate(quads):
                    t0, k = quad[0][0], len(quad)
                    act.wait_ge(zf_ready, n + 1)
                    nc.scalar.copy(z_hi[:, t0:t0 + k], z_f[:, t0:t0 + k]).then_inc(zhi_ready, 1)
                    if n:
                        lo_half(nc, act, n - 1)
                lo_half(nc, act, len(quads) - 1)
                for n, (a, width) in enumerate(blocks):
                    if n + 1 < len(blocks):
                        a1, width1 = blocks[n + 1]
                        if n >= 1:
                            act.wait_ge(agg_ready, n)
                        nc.scalar.copy(cnt16[:, (n + 1) % 2, 0:ACT_ROWS, 0:width1],
                                       count[:, 0:ACT_ROWS, a1:a1 + width1]).then_inc(cv_act, 1)
                    act.wait_ge(agg_ready, n + 1)
                    nc.scalar.copy(xt[:, a:a + width], bank[n % 2][:, 0:width]).then_inc(agg_copied, 1)
                    if n:
                        deviation(nc, act, n - 1)
                deviation(nc, act, len(blocks) - 1)
            with act.Else():
                for n in range(len(blocks)):
                    deviation(nc, act, n)

        @block.vector
        def _(v):
            nd = [0]

            def chain(ins):
                nd[0] += 1
                ins.then_inc(dve, 1)
                v.wait_ge(dve, nd[0])

            nc.vector.memset(x_nm[:, full, :], 0.0).then_inc(tail_zero, 1)
            nc.vector.memset(wcomp_bd[:], 0.0).then_inc(wbd_zero, 1)
            nc.vector.memset(eps_col[:], EPS)
            nc.vector.memset(ones16[:], 1.0)
            nc.vector.memset(ones32[:], 1.0)
            for padded in (neg_lo, rel, norm):
                nc.vector.memset(padded[:, CHUNKS:], 0.0)
            nc.vector.memset(deg[:], 1.0)
            nc.vector.memset(mv[:], 1.0)
            nc.vector.memset(acc[:, NODES:], 0.0).then_inc(rows_added, 1)
            nc.vector.memset(g_sb[:], 0.0).then_inc(g_taken, 4)
            v.wait_ge(iotas, 1)
            chain(nc.vector.tensor_scalar(rel_id_i[:], lane_i[:], RELS - 1, None, ALU.bitwise_and))
            nc.vector.tensor_copy(rel_id[:], rel_id_i[:])
            v.wait_ge(ld_edges, 80)
            chain(nc.vector.tensor_scalar(work_i, src_i, P - 1, None, ALU.bitwise_and))
            chain(nc.vector.tensor_scalar(neg_lo[:, 0:CHUNKS], work_i, -1.0, None, ALU.mult))
            nc.vector.tensor_scalar(work_i, src_i, 7, None, ALU.logical_shift_right).then_inc(nums_ready, 1)
            v.wait_ge(nums_ready, 1)
            chain(nc.vector.tensor_tensor(rel[:, 0:CHUNKS], dst_i, start_b, ALU.subtract))
            chain(nc.vector.scalar_tensor_tensor(key[:], work_i, float(WIN), rel[:, 0:CHUNKS], ALU.mult, ALU.add))

            def type_one_hot(i):
                v.wait_ge(typ_loaded, 64 * i + 64)
                nc.vector.tensor_scalar(typ_oh[:], typ[:], rel_id[:], None, ALU.is_equal).then_inc(typ_done, 1)

            type_one_hot(0)
            tests = h_nm[:].rearrange("p t f -> p (t f)")[:, 4 * CHUNKS:7 * CHUNKS + 1]
            n = CHUNKS - 1
            nc.vector.tensor_copy(lane[:], lane_i[:])
            chain(nc.vector.tensor_scalar(least[:], lane_i[:], P - 1, None, ALU.is_equal))
            nc.vector.tensor_scalar(spare[:], lane[:], float(NODES), None, ALU.add)
            nc.vector.tensor_scalar(tests[:, 0:CHUNKS], rel[:, 0:CHUNKS], float(WIN), None, ALU.is_ge)
            nc.vector.tensor_scalar(tests[:, CHUNKS:CHUNKS + n], rel[:, 0:n], least[:], None, ALU.is_lt)
            nc.vector.tensor_tensor(tests[:, CHUNKS + n:CHUNKS + 2 * n], dst_i[:, 0:n], start_b[:, 1:CHUNKS], ALU.is_gt)
            chain(nc.vector.tensor_scalar(tests[:, 3 * CHUNKS:3 * CHUNKS + 1], dst_i[:, n:CHUNKS], 0.0, None, ALU.is_ge))
            chain(nc.vector.scalar_tensor_tensor(tests[:, CHUNKS + 2 * n:CHUNKS + 2 * n + 1], rel[:, n:CHUNKS], 0.0,
                                                 tests[:, 3 * CHUNKS:3 * CHUNKS + 1], ALU.is_lt, ALU.mult))
            nc.vector.tensor_reduce(bad[:], tests[:, 0:CHUNKS + 2 * n + 1], AX.X, ALU.max).then_inc(bad_ready, 1)
            v.wait_ge(bad_summed, 1)
            nc.vector.tensor_scalar(flag[:], bank[7][0:1, 0:1], 1.0, None, ALU.min).then_inc(flag_ready, 1)
            nc.vector.memset(count[:].rearrange("p a b -> p (a b)").bitcast(mybir.dt.uint32), 0).then_inc(counts_added, 1)
            v.wait_ge(counts_added, 1)
            v.wait_ge(iotas, 3)
            squares = count[:].rearrange("p r n -> p (r n)")[:, 0:full * (NPAD + P)].rearrange("p (t w) -> p t w", t=full)
            nc.vector.tensor_copy(squares[:, :, 0:P], ident[:].unsqueeze(1).broadcast_to([P, full, P]))
            nc.vector.tensor_copy(count[:, full, full * P:NODES], ident[:, 0:LAST]).then_inc(counts_added, 1)
            v.wait_ge(counts_added, 2)
            v.wait_ge(init_taken, len(blocks))

            def add_counts(start, c, j, n):
                v.wait_ge(cnt_ready, c)
                v.wait_ge(counts_added, n)
                w = count[:, :, bass.ds(start, WIN)]
                nc.vector.tensor_tensor(w, w, cnt_ps[j % 4][:, 0:ROWS * WIN].rearrange("p (r n) -> p r n", n=WIN),
                                        ALU.add).then_inc(counts_added, 1)

            def add_rows(start, h, k, n):
                v.wait_ge(rows_added, n)
                w = acc[:, bass.ds(start, WIN)]
                nc.vector.tensor_tensor(w, w, z_ps[h][:, k * WIN:(k + 1) * WIN], ALU.add).then_inc(rows_added, 1)

            def load_starts(at, n):
                _, vals = nc.values_load_multi_w_load_instructions(
                    start_i[0:1, bass.ds(at, n)], engines=[mybir.EngineType.DVE], min_val=0, max_val=NODES - 1,
                    skip_runtime_bounds_check_because="window starts are destination nodes, below 3125")
                return vals

            def coefficients(i):
                v.wait_ge(coef_copied, i + 1)
                nc.vector.tensor_tensor(
                    coef[:].rearrange("p (q j) b -> p q j b", q=Q),
                    coef_raw[:].rearrange("p (j q b) -> p q j b", q=Q, b=BASES),
                    norm[:, bass.ds(STEP * i, STEP)].rearrange("p (q j) -> p q j", q=Q).unsqueeze(3).broadcast_to([P, Q, Q, BASES]),
                    ALU.mult).then_inc(coef_taken, 1)

            def window_one_hot(g, h):
                nc.vector.tensor_tensor(
                    win_oh[:, h], iota_key[:, 0:WIN].unsqueeze(1).broadcast_to([P, GROUP, WIN]),
                    rel[:, bass.ds(GROUP * g, GROUP)].unsqueeze(2).broadcast_to([P, GROUP, WIN]),
                    ALU.is_equal).then_inc(win_ready, 1)

            def scatter(g, h, steps_taken):
                v.wait_ge(win_ready, g + 1)
                v.wait_ge(coef_taken, steps_taken)
                nc.vector.tensor_tensor(
                    scat[:, h], win_oh[:, h].unsqueeze(2).broadcast_to([P, GROUP, BASES, WIN]),
                    coef[:, GROUP * h:GROUP * (h + 1), :].unsqueeze(3).broadcast_to([P, GROUP, BASES, WIN]),
                    ALU.mult).then_inc(scat_ready, 1)

            narrow = is_narrow(v)
            with v.If(narrow):
                coefficients(0)
                window_one_hot(0, 0)
                scatter(0, 0, 1)
                with v.Fori(0, STEPS) as i:
                    for h in range(2):
                        g = 2 * i + h
                        a_start = load_starts(GROUP * g, GROUP)
                        c_start = load_starts(GROUP * g + LEAD - LAG, GROUP)
                        for j in range(GROUP):
                            c = GROUP * g + j
                            nc.vector.tensor_scalar(key_oh[:, h, j, 0:KEYS], iota_key[:], key[:, bass.ds(c, 1)], None,
                                                    ALU.is_equal).then_inc(key_ready, 1)
                            if j == 0:
                                v.wait_ge(z_ready, g + 1)
                            add_rows(a_start[j], h, j, c + 1)
                            add_counts(c_start[j], c + 1, j - LAG, c + 2)
                            if j == 0 and h == 0:
                                type_one_hot(i + 1)
                            if j == 3 and h == 1:
                                coefficients(i + 1)
                            if j == 3:
                                window_one_hot(g + 1, 1 - h)
                            if j == 4:
                                scatter(g + 1, 1 - h, i + 1 + h)
                c_start = load_starts(CHUNKS + LEAD - LAG, LAG)
                for k in range(LAG):
                    add_counts(c_start[k], CHUNKS + k + 1, k - LAG, CHUNKS + k + 2)
                n = CHUNKS + 1
                for g in (2 * STEPS, 2 * STEPS + 1):
                    a_start = load_starts(GROUP * g, GROUP)
                    v.wait_ge(z_ready, g + 1)
                    for k in range(GROUP):
                        add_rows(a_start[k], g % 2, k, n)
                        n += 1
                v.wait_ge(rows_added, n)
                v.wait_ge(counts_added, CHUNKS + LAG + 2)
                nc.vector.tensor_copy(deg_part, count[:, TILES, :]).then_inc(deg_ready, 1)
                v.wait_ge(degt_ready, 1)
                nc.vector.tensor_scalar(deg[:, 0:full], bank[7][:, 0:full], 1.0, None, ALU.add)
                nc.vector.tensor_scalar(deg[0:LAST, full:TILES], bank[7][0:LAST, full:TILES], 1.0, None,
                                        ALU.add).then_inc(sums_ready, 1)
            with v.Else():
                general_vector(v, 0)
                nc.vector.engine_nop().then_inc(sums_ready, 1)
            v.wait_ge(sums_ready, 1)
            nc.vector.engine_nop().then_inc(deg_taken, 1)
            done = [0]

            def link(ins):
                done[0] += 1
                ins.then_inc(tail, 1)
                v.wait_ge(tail, done[0])

            def flat(ap):
                return ap.rearrange("p a b -> p (a b)")

            for n, quad in enumerate(quads):
                v.wait_ge(t_ready, n + 1)
                t0, k, r = quad[0][0], len(quad), quad[0][1]
                nc.vector.scalar_tensor_tensor(
                    flat(x_nm[0:r, t0:t0 + k, :]), bank[n % 4][0:r, 0:k * FEAT], 0.0, flat(x_nm[0:r, t0:t0 + k, :]),
                    ALU.max, ALU.add).then_inc(t_taken, 1)
                v.wait_ge(t_taken, n + 1)
                for t, r in quad:
                    ins = nc.vector.bn_stats(stats[0:r, t, :], x_nm[0:r, t, :])
                link(ins)
                for t, r in quad:
                    ins = nc.vector.bn_aggr(mv[0:r, t, :], stats[0:r, t, :])
            link(ins)
            nc.vector.engine_nop().then_inc(var_ready, 1)
            v.wait_ge(sd_ready, 1)
            link(nc.vector.reciprocal(dinv[:], dinv[:]))
            v.wait_ge(sd_ready, 2)
            link(nc.vector.reciprocal(rstd[:], sdev[:]))
            link(nc.vector.tensor_tensor(scale_z[:], rstd[:], dinv[:], ALU.mult))

            def z_rest(n):
                t0, k = quads[n][0][0], len(quads[n])
                v.wait_ge(zhi_ready, n + 1)
                nc.vector.tensor_tensor(flat(z_f[:, t0:t0 + k]), flat(z_f[:, t0:t0 + k]), flat(z_hi[:, t0:t0 + k]),
                                        ALU.subtract).then_inc(zd_ready, 1)

            def convert(n):
                a, width = blocks[n]
                if n >= 2:
                    v.wait_ge(agg_ready, n - 1)
                nc.vector.tensor_copy(cnt16[:, n % 2, ACT_ROWS:TILES, 0:width],
                                      count[:, ACT_ROWS:TILES, a:a + width]).then_inc(cv_dve, 1)

            def residual():
                for t, r in tiles:
                    ins = nc.vector.tensor_scalar(h_nm[:, t, :], x_nm[:, t, :], mv[:, t, 0:1], rstd[:, t:t + 1],
                                                  ALU.subtract, ALU.mult)
                link(ins)
                v.wait_ge(ld_w, 16 * (Q + 3))
                link(nc.vector.tensor_tensor(h_nm[:], h_nm[:], bias1_b[:].unsqueeze(1).broadcast_to([P, TILES, FEAT]), ALU.add))

            def finish(n):
                quad = quads[n]
                t0, k = quad[0][0], len(quad)
                v.wait_ge(fin_ready, n + 1)
                for t, r in quad:
                    ins = nc.vector.scalar_tensor_tensor(
                        h_nm[0:r, t, :], bank[4 + n % 2][0:r, (t - t0) * FEAT:(t - t0 + 1) * FEAT], dinv[0:r, t:t + 1],
                        h_nm[0:r, t, :], ALU.mult, ALU.add)
                link(ins)
                nc.vector.engine_nop().then_inc(fin_taken, 1)
                for t, r in quad:
                    ins = nc.vector.bn_stats(stats[0:r, t, :], h_nm[0:r, t, :])
                link(ins)
                for t, r in quad:
                    ins = nc.vector.bn_aggr(mv[0:r, t, :], stats[0:r, t, :])
                ins.then_inc(var1, 1)
                v.wait_ge(sd1, n + 1)
                link(nc.vector.reciprocal(rstd[:, t0:t0 + k], sdev[:, t0:t0 + k]))
                for t, r in quad:
                    ins = nc.vector.tensor_scalar(x_nm[0:r, t, :], h_nm[0:r, t, :], mv[0:r, t, 0:1], rstd[0:r, t:t + 1],
                                                  ALU.subtract, ALU.mult)
                ins.then_inc(out_ready, 1)

            links_before = done[0]
            with v.If(narrow):
                for n, quad in enumerate(quads):
                    for t, r in quad:
                        ins = nc.vector.tensor_scalar(z_f[:, t, :], x_nm[:, t, :], mv[:, t, 0:1], scale_z[:, t:t + 1],
                                                      ALU.subtract, ALU.mult)
                    ins.then_inc(zf_ready, 1)
                    if n:
                        z_rest(n - 1)
                z_rest(len(quads) - 1)
                convert(1)
                residual()
                for n, (a, width) in enumerate(blocks):
                    if n + 2 < len(blocks):
                        convert(n + 2)
                    v.wait_ge(agg_copied, n + 1)
                    nc.vector.scalar_tensor_tensor(acc[:, a:a + width], bank[2 + n % 2][:, 0:width], 1.0 / LOSCALE,
                                                   xt[:, a:a + width], ALU.mult, ALU.add).then_inc(agg_done, 1)
                    if n:
                        finish(n - 1)
                finish(len(blocks) - 1)
            with v.Else():
                done[0] = links_before
                residual()
                general_vector(v, 1)
                nc.vector.engine_nop().then_inc(agg_done, len(blocks))
                for n in range(len(blocks)):
                    finish(n)

        @block.tensor
        def _(pe):
            pe.wait_ge(iotas, 3)
            pe.wait_ge(ld_x, 64)
            for n, quad in enumerate(quads):
                if n >= 2:
                    pe.wait_ge(xt_taken, n - 1)
                for t, r in quad:
                    c = (t - quad[0][0]) * P
                    last = nc.tensor.transpose(bank[n % 2][:, c:c + r], x_nm[0:r, t, :], ident[0:r, 0:r])
                last.then_inc(xt_ready, 1)
            for n, (a, width) in enumerate(blocks):
                pe.wait_ge(xt_taken, n + 1)
                if n >= 2:
                    pe.wait_ge(init_taken, n - 1)
                nc.tensor.matmul(bank[2 + n % 2][:, 0:width], loop_sb[:], xt[:, a:a + width],
                                 start=True, stop=True).then_inc(init_ready, 1)

            def second_product(h, b):
                last = nc.tensor.matmul(z_ps[h][:, 0:GROUP * WIN], wt[:, b, :], g_sb[:, h, b, :],
                                        start=(b == 0), stop=(b == BASES - 1))
                if b == BASES - 1:
                    last.then_inc(z_ready, 1)

            def look_up(i):
                pe.wait_ge(typ_done, i + 1)
                for j in range(Q):
                    at = (Q - 1 - j) * Q * BASES
                    last = nc.tensor.matmul(coef_ps[:], typ_oh[:, j, :], wcomp_bd[:, at:at + Q * Q * BASES],
                                            start=(j == 0), stop=(j == Q - 1))
                return last

            pe.wait_ge(ld_w, 16 * (Q + 3))
            pe.wait_ge(bad_ready, 1)
            nc.tensor.matmul(bank[7][0:1, 0:1], bad[:], ones32[:], start=True, stop=True).then_inc(bad_summed, 1)
            narrow = is_narrow(pe)
            pe.wait_ge(init_taken, len(blocks))
            with pe.If(narrow):
                look_up(0).then_inc(coef_ready, 1)
                pe.wait_ge(coef_copied, 1)
                pe.wait_ge(g_taken, 4)
                for b in range(BASES):
                    second_product(0, b)
                pe.wait_ge(init_taken, len(blocks))
                zeros = g_sb[:, 0].rearrange("p b n -> p (b n)")
                for k in range(LAG):
                    nc.tensor.matmul(cnt_ps[4 - LAG + k][:, 0:ROWS * WIN], zeros[:, 0:P], zeros[:, 0:ROWS * WIN],
                                     start=True, stop=True).then_inc(cnt_ready, 1)
                with pe.Fori(0, STEPS) as i:
                    for h in range(2):
                        g = 2 * i + h
                        for j in range(GROUP):
                            q, jj, c = j // 4, j % 4, GROUP * g + j
                            if j == 0:
                                pe.wait_ge(scat_ready, g + 1)
                            if jj == 0:
                                pe.wait_ge(g_taken, 2 * g + q + 3)
                            if j == 4 and h == 0:
                                look_up(i + 1)
                            pe.wait_ge(gathered[GROUP * h + j], 16 * i + 16)
                            last = nc.tensor.matmul(g_ps[q][:, jj * BASES * WIN:(jj + 1) * BASES * WIN],
                                                    rows[:, GROUP * h + j, :],
                                                    scat[:, h, j].rearrange("p b n -> p (b n)"), start=True, stop=True)
                            if jj == 3:
                                last.then_inc(g_ready, 1)
                            if j == 1:
                                pe.wait_ge(g_taken, 2 * g + 4)
                                pe.wait_ge(rows_added, GROUP * g + 1)
                            for b in range(BASES)[max(j - 1, 0):j + j // (GROUP - 1)]:
                                second_product(1 - h, b)
                            pe.wait_ge(key_ready, c + 1)
                            if j == 0:
                                pe.wait_ge(lo_ready, g + 1)
                            pe.wait_ge(counts_added, c + 1)
                            nc.tensor.matmul(cnt_ps[j % 4][:, 0:KEYS + WIN], lo_oh[:, h, j, :], key_oh[:, h, j, :],
                                             start=True, stop=True).then_inc(cnt_ready, 1)
                pe.wait_ge(g_taken, 4 * STEPS + 4)
                pe.wait_ge(rows_added, CHUNKS + 1)
                for b in range(BASES):
                    second_product(1, b)
                pe.wait_ge(deg_ready, 1)
                for t, r in tiles:
                    last = nc.tensor.matmul(bank[7][0:r, t:t + 1], deg_part[:, t * P:t * P + r], ones16[:, 0:1],
                                            start=True, stop=True)
                last.then_inc(degt_ready, 1)
            with pe.Else():
                general_tensor(pe, 0)
            pe.wait_ge(sums_ready, 1)
            for n, quad in enumerate(quads):
                if n >= 4:
                    pe.wait_ge(t_taken, n - 3)
                for t, r in quad:
                    c = (t - quad[0][0]) * P
                    last = nc.tensor.transpose(bank[n % 4][0:r, c:c + P], acc[:, t * P:t * P + r], ident[:])
                last.then_inc(t_ready, 1)

            def project(n):
                pe.wait_ge(agg_done, n + 1)
                if n >= 2:
                    pe.wait_ge(fin_taken, n - 1)
                for t, r in quads[n]:
                    c = (t - quads[n][0][0]) * FEAT
                    last = nc.tensor.matmul(bank[4 + n % 2][0:r, c:c + FEAT], acc[:, t * P:t * P + r], w1_sb[:],
                                            start=True, stop=True)
                last.then_inc(fin_ready, 1)

            with pe.If(narrow):
                pe.wait_ge(zlo_ready, len(quads))
                for n, (a, width) in enumerate(blocks):
                    pe.wait_ge(cv_act, n + 1)
                    if n:
                        pe.wait_ge(cv_dve, n)
                    if n >= 2:
                        pe.wait_ge(agg_done, n - 1)
                    for t in range(TILES):
                        for half, to in ((z_hi, 0), (z_lo, 2)):
                            last = nc.tensor.matmul(bank[to + n % 2][:, 0:width], half[:, t, :], cnt16[:, n % 2, t, 0:width],
                                                    start=(t == 0), stop=(t == TILES - 1))
                    last.then_inc(agg_ready, 1)
                    if n:
                        project(n - 1)
                project(len(blocks) - 1)
            with pe.Else():
                general_tensor(pe, 1)
                for n in range(len(blocks)):
                    project(n)


def kernel(x, src, dst, edge_type_32, edge_weight1, L0_gnn_weight, L0_gnn_w_comp, L0_gnn_loop_weight,
           L0_gnn_h_bias, L1_gnn_W, L1_gnn_b):
    import numpy as np
    import concourse.bacc as bacc
    from concourse.bass_utils import run_bass_kernel_spmd

    def arr(a):
        return np.ascontiguousarray(a)

    pad = CHUNKS * P - EDGES
    src, dst, types = (np.asarray(a) for a in (src, dst, edge_type_32))
    src_p = np.pad(src, (0, pad)).reshape(CHUNKS, P)
    dst_p = np.pad(dst, (0, pad), constant_values=-1).reshape(CHUNKS, P)
    norm_p = np.pad(np.asarray(edge_weight1)[:, 0], (0, pad)).reshape(CHUNKS, P)
    step = STEP * P
    arrays = {
        "x": arr(x),
        "src_idx": arr(np.pad(src_p, ((0, STEP), (0, 0))).reshape(STEPS + 1, 2, GROUP, P).transpose(0, 1, 3, 2)),
        "src_t": arr(src_p.T), "dst_t": arr(dst_p.T), "src_rows": arr(src_p), "dst_rows": arr(dst_p),
        "starts": arr(np.pad(dst[::P], (LEAD, 0))[None]),
        "types": arr(np.pad(types, (0, pad + step)).reshape(STEPS + 1, Q, 1, Q * P)),
        "type_rows": arr(np.pad(types, (0, pad)).reshape(CHUNKS, P)),
        "norm_t": arr(norm_p.T),
        "weight": arr(L0_gnn_weight), "w_comp": arr(L0_gnn_w_comp), "loop_w": arr(L0_gnn_loop_weight),
        "bias0": arr(L0_gnn_h_bias), "w1": arr(L1_gnn_W), "bias1": arr(L1_gnn_b),
    }
    nc = bacc.Bacc("TRN2", target_bir_lowering=False, num_devices=1)
    args = [nc.dram_tensor(name, a.shape, mybir.dt.from_np(a.dtype), kind="ExternalInput").ap()
            for name, a in arrays.items()]
    out = nc.dram_tensor("out", (NODES, FEAT), F32, kind="ExternalOutput").ap()
    gnn_kernel(nc, *args, out)
    result = run_bass_kernel_spmd(nc, [arrays], core_ids=[0])
    return result.results[0]["out"]
```

```python
from contextlib import ExitStack

import concourse.bass as bass
import concourse.mybir as mybir

F32, F16, I32, U8 = mybir.dt.float32, mybir.dt.float16, mybir.dt.int32, mybir.dt.uint8
ALU = mybir.AluOpType
ACT = mybir.ActivationFunctionType
AX = mybir.AxisListType

P = 128
NODES, FEAT, EDGES, RELS, BASES = 3125, 128, 53125, 32, 8
CHUNKS = -(-EDGES // P)
GROUP = 8
STEP = 2 * GROUP
STEPS = CHUNKS // STEP
WIN = 12
TILES = -(-NODES // P)
LAST = NODES - (TILES - 1) * P
NPAD = 3136
KEYS = TILES * WIN
ROWS = TILES + 1
LEAD = STEP
LAG = 2
EPS = 1e-5
ACT_ROWS = 14
FIRST_ROWS, FIRST_DVE = 15, 4
ZSCALE = 2048.0
ZERO_POOL, ZERO_ACT, ZERO_DVE = 1600, 8400, 4800
Q = P // RELS
BLOCK = 512


def gnn_kernel(nc, x, src_idx, src_t, dst_t, src_rows, dst_rows, starts, types, type_rows, norm_t, weight, w_comp, loop_w,
               bias0, w1, bias1, out):
    ctx = ExitStack()
    with ctx:
        def sb(name, shape, dt):
            return ctx.enter_context(nc.sbuf_tensor(name, shape, dt))

        def sem(name):
            return ctx.enter_context(nc.semaphore(name))

        cnt16 = sb("cnt16", [P, 2, TILES, BLOCK], F16)
        arena, used = cnt16[:].rearrange("p a b c -> p (a b c)"), [0]

        def carve(dims, dt, size):
            n = 1
            for d in dims:
                n *= d
            at, used[0] = used[0], used[0] + -(-n * size // 64) * 32
            assert used[0] <= 2 * TILES * BLOCK
            flat = arena[:, at:at + n * size // 2]
            flat = flat if dt == F16 else flat.bitcast(dt)
            names = "abcd"[:len(dims)]
            return flat.rearrange(f"p ({' '.join(names)}) -> p {' '.join(names)}", **dict(zip(names[1:], dims[1:])))

        x_nm = sb("x_nm", [P, TILES, FEAT], F32)
        norm = carve([CHUNKS + STEP], F32, 4)
        start_i = sb("start_i", [1, LEAD + CHUNKS], I32)
        wt = sb("wt", [FEAT, BASES, FEAT], F32)
        wcomp_bd = sb("wcomp_bd", [P, (2 * Q - 1) * Q * BASES], F32)
        loop_sb = sb("loop_sb", [FEAT, FEAT], F32)
        w1_sb = sb("w1_sb", [FEAT, FEAT], F32)
        bias0_col = sb("bias0_col", [FEAT, 1], F32)
        bias1_b = sb("bias1_b", [P, FEAT], F32)
        ident = sb("ident", [P, P], F32)
        iota_lo = sb("iota_lo", [P, P], F16)
        iota_key = sb("iota_key", [P, KEYS], F16)
        rel_id = sb("rel_id", [P, 1], F32)
        lane_i = sb("lane_i", [P, 1], I32)
        rel_id_i = sb("rel_id_i", [P, 1], I32)
        ones16 = sb("ones16", [P, 1], F16)
        eps_col = sb("eps_col", [P, 1], F32)
        neg_lo = sb("neg_lo", [P, CHUNKS + STEP], F32)
        rel = carve([CHUNKS + STEP], F32, 4)
        key = carve([CHUNKS], F32, 4)
        idx = sb("idx", [P, 2, GROUP], I32)
        rows = carve([STEP, FEAT], F32, 4)
        typ = carve([Q, P], I32, 4)
        typ_oh = carve([Q, P], F32, 4)
        coef_raw = carve([STEP * BASES], F32, 4)
        coef = carve([STEP, BASES], F32, 4)
        scat = carve([2, GROUP, BASES, WIN], F32, 4)
        key_oh = carve([2, GROUP, KEYS + WIN], F16, 2)
        win_oh = key_oh[:, :, :, KEYS:]
        lo_abs = carve([GROUP, P], F16, 2)
        lo_oh = carve([2, GROUP, P], F16, 2)
        g_sb = carve([2, BASES, GROUP * WIN], F32, 4)
        count = sb("count", [P, ROWS, NPAD], U8)
        acc = sb("acc", [FEAT, NPAD], F32)
        xt = sb("xt", [FEAT, TILES * P], F32)
        e_src, e_dst, e_to = sb("e_src", [P, 1], I32), sb("e_dst", [P, 1], I32), sb("e_to", [P, 1], I32)
        e_dstf, e_flag, e_far = sb("e_dstf", [P, 1], F32), sb("e_flag", [P, 1], F32), sb("e_far", [P, 1], F32)
        e_coef = sb("e_coef", [P, BASES], F32)
        lane, spare, least = sb("lane", [P, 1], F32), sb("spare", [P, 1], F32), sb("least", [P, 1], F32)
        tests, zero_col = sb("tests", [P, 4], F32), sb("zero_col", [P, 1], F32)
        shift_z = sb("shift_z", [P, TILES], F32)
        bad, ones32, flag = sb("bad", [P, 1], F32), sb("ones32", [P, 1], F32), sb("flag", [1, 1], I32)
        deg = sb("deg", [P, TILES], F32)
        dinv = sb("dinv", [P, TILES], F32)
        h_nm = sb("h_nm", [P, TILES, FEAT], F32)
        early = h_nm[:].rearrange("p t f -> p (t f)")[:, 0:4 * CHUNKS].bitcast(I32).rearrange("p (a k) -> p a k", a=4)
        src_i, dst_i, start_b, work_i = (early[:, n] for n in range(4))
        z_hi = sb("z_hi", [P, TILES, FEAT], F16)
        deg_part = z_hi[:].rearrange("p t f -> p (t f)")[:, 0:NPAD]
        z_lo = sb("z_lo", [P, TILES, FEAT], F16)
        stats = sb("stats", [P, TILES, 6], F32)
        mv = sb("mv", [P, TILES, 2], F32)
        rstd = sb("rstd", [P, TILES], F32)
        sdev = sb("sdev", [P, TILES], F32)
        scale_z = sb("scale_z", [P, TILES], F32)
        z_f = xt[:].rearrange("p (t f) -> p t f", f=FEAT)

        bank = [ctx.enter_context(nc.psum_tensor(f"bank{n}", [P, 512], F32)) for n in range(8)]
        cnt_ps, g_ps, z_ps = bank[0:4], bank[4:6], bank[6:8]
        coef_ps = g_ps[1][:, 4 * BASES * WIN:]

        def s16(n):
            return [sem(f"{n}{k}") for k in range(STEP)]
        gathered = s16("gathered")
        slot_free = sem("slot_free")
        idx_loaded = [sem("idx_loaded0"), sem("idx_loaded1")]
        ld_edges, ld_loop, ld_w = sem("ld_edges"), sem("ld_loop"), sem("ld_w")
        ld_x = [sem(f"ld_x{k}") for k in range(4)]
        win_ready = sem("win_ready")
        typ_loaded, typ_done = sem("typ_loaded"), sem("typ_done")
        coef_ready, coef_copied, coef_taken = sem("coef_ready"), sem("coef_copied"), sem("coef_taken")
        iotas, wbd_zero, tail_zero = sem("iotas"), sem("wbd_zero"), sem("tail_zero")
        dve, counts_added, rows_added = sem("dve"), sem("counts_added"), sem("rows_added")
        nums_ready = sem("nums_ready")
        scat_ready, key_ready, lo_ready, lo_step = sem("scat_ready"), sem("key_ready"), sem("lo_ready"), sem("lo_step")
        g_ready, g_taken, cnt_ready = sem("g_ready"), sem("g_taken"), sem("cnt_ready")
        z_ready = sem("z_ready")
        xt_ready, xt_taken, init_ready, init_taken = sem("xt_ready"), sem("xt_taken"), sem("init_ready"), sem("init_taken")
        deg_ready, degt_ready, t_ready, t_taken = sem("deg_ready"), sem("degt_ready"), sem("t_ready"), sem("t_taken")
        deg_taken, var_ready, sd_ready, tail = sem("deg_taken"), sem("var_ready"), sem("sd_ready"), sem("tail")
        zf_ready, zhi_ready, zd_ready, zlo_ready = sem("zf_ready"), sem("zhi_ready"), sem("zd_ready"), sem("zlo_ready")
        cv_dve, cv_act = sem("cv_dve"), sem("cv_act")
        agg_ready, agg_copied, agg_done = sem("agg_ready"), sem("agg_copied"), sem("agg_done")
        fin_ready, fin_taken, var1, sd1, out_ready, stored = sem("fin_ready"), sem("fin_taken"), sem("var1"), sem("sd1"), sem("out_ready"), sem("stored")

        zeroed, zero_ready, ld_norm = sem("zeroed"), sem("zero_ready"), sem("ld_norm")
        dinv_sqrt, scale_ready, h_ready, res_ready = sem("dinv_sqrt"), sem("scale_ready"), sem("h_ready"), sem("res_ready")
        cv_first, cv_first_dve = sem("cv_first"), sem("cv_first_dve")
        flag_ready, bad_ready, bad_summed = sem("flag_ready"), sem("bad_ready"), sem("bad_summed")
        sums_ready = sem("sums_ready")
        events = ("loaded", "gathered", "turned", "xt", "types", "products", "message", "to", "summed", "total",
                  "added", "chunk_free", "cleared", "z", "dve", "back", "back_turned", "back_added", "back_taken")
        general = [{e: sem(f"general{n}_{e}") for e in events} for n in range(2)]
        general[0]["clears"], general[1]["clears"] = TILES + 1, 2 * TILES + 1
        sums = [nc.dram_tensor(f"sums{n}", (NODES + P, FEAT + 1 - n), F32, kind="Internal").ap() for n in range(2)]
        z_dram = nc.dram_tensor("z_dram", (NODES, FEAT), F32, kind="Internal").ap()
        e_rows, e_xt, same, earlier, before = (rows[:, n] for n in range(5))
        dst_row, e_typ, e_typ_oh = rows[:, 5].bitcast(I32), rows[0:RELS, 6].bitcast(I32), rows[0:RELS, 7]
        pair = rows[:].rearrange("p (a b) f -> p a (b f)", b=2)
        message, total = pair[:, 4], pair[:, 5]

        full = TILES - 1
        tiles = [(t, P if t < full else LAST) for t in range(TILES)]
        cuts = [0, 4, 8, 12, 16, 20, 23, TILES]
        quads = [tiles[a:b] for a, b in zip(cuts, cuts[1:])]
        blocks = [(q[0][0] * P, sum(r for _, r in q)) for q in quads]

        block = ctx.enter_context(nc.Block())

        x_parts = [(0, 8), (8, 16), (16, full)]
        count_words = count[:].rearrange("p a b -> p (a b)").bitcast(F32)

        def is_narrow(eng):
            eng.wait_ge(flag_ready, 1)
            return eng.value_load(flag[0:1, 0:1], min_val=0, max_val=1) == 0

        def general_sync(sp, layer):
            g = general[layer]
            if layer == 0:
                source = h_nm[:].rearrange("p t f -> p (t f)")[:, 0:FEAT + 1]
                sp.wait_ge(g["z"], 1)
                for t in range(TILES + 1):
                    r = min(P, NODES + P - t * P)
                    sp.dma_start(sums[0][t * P:t * P + r, :], source[0:r, :]).then_inc(g["cleared"], 16)
            else:
                sp.wait_ge(zf_ready, len(quads))
                for t, r in tiles:
                    sp.dma_start(sums[1][t * P:t * P + r, :], z_f[0:r, t, :]).then_inc(g["cleared"], 16)
                    sp.dma_start(z_dram[t * P:t * P + r, :], z_f[0:r, t, :]).then_inc(g["cleared"], 16)
                sp.dma_start(sums[1][NODES:NODES + P, :], z_f[:, 0, :]).then_inc(g["cleared"], 16)
            sp.wait_ge(g["cleared"], 16 * g["clears"])
            sp.sem_inc(g["chunk_free"], 1)
            with sp.Fori(0, CHUNKS) as k:
                sp.wait_ge(g["chunk_free"], k + 1)
                sp.dma_start(e_src[:], src_rows[bass.ds(k, 1), :].rearrange("o p -> p o")).then_inc(g["loaded"], 16)
                sp.dma_start(e_dst[:], dst_rows[bass.ds(k, 1), :].rearrange("o p -> p o")).then_inc(g["loaded"], 16)
                sp.dma_start(dst_row, dst_rows[bass.ds(k, 1), :].broadcast_to([P, P])).then_inc(g["loaded"], 16)
                sp.dma_start(e_typ, type_rows[bass.ds(k, 1), :].broadcast_to([RELS, P])).then_inc(g["loaded"], 16)
            sp.wait_ge(g["chunk_free"], CHUNKS + 1)
            width = FEAT + 1 - layer
            for t, r in tiles:
                if t:
                    sp.wait_ge(g["back_taken"], t)
                sp.dma_start(total[0:r, 0:width], sums[layer][t * P:t * P + r, :]).then_inc(g["back"], 16)

        def general_gpsimd(pool, layer):
            g = general[layer]
            table, rows_in = (x, e_rows) if layer == 0 else (z_dram, message[:, 0:FEAT])
            width = FEAT + 1 - layer
            with pool.Fori(0, CHUNKS) as k:
                pool.wait_ge(g["loaded"], 64 * k + 64)
                pool.sem_inc(slot_free, 1)
                pool.indirect_dma_start(rows_in, None, table[:, :],
                                        bass.IndirectOffsetOnAxis(ap=e_src[:], axis=0)).then_inc(g["gathered"], 16)
                pool.wait_ge(g["total"], k + 1)
                pool.sem_inc(slot_free, 1)
                pool.indirect_dma_start(sums[layer][:, :], bass.IndirectOffsetOnAxis(ap=e_to[:], axis=0),
                                        total[:, 0:width], None, compute_op=ALU.add).then_inc(g["added"], 16)
                pool.wait_ge(g["added"], 16 * k + 16)
                pool.sem_inc(g["chunk_free"], 1)

        def general_scalar(act, layer):
            g = general[layer]
            if layer == 0:
                with act.Fori(0, CHUNKS) as k:
                    act.wait_ge(g["turned"], k + 1)
                    nc.scalar.copy(e_xt, bank[0][:, 0:P]).then_inc(g["xt"], 1)

        def general_vector(v, layer):
            g = general[layer]
            width = FEAT + 1 - layer
            if layer == 0:
                nc.vector.memset(h_nm[:, 0:2, :], 0.0).then_inc(g["z"], 1)
            nc.vector.tensor_scalar(before, iota_lo[:], lane[:], None, ALU.is_lt).then_inc(g["dve"], 1)
            with v.Fori(0, CHUNKS) as k:
                n = [0]

                def link(ins):
                    n[0] += 1
                    ins.then_inc(g["dve"], 1)
                    v.wait_ge(g["dve"], steps * k + n[0] + 1)
                steps = 6 + (1 + BASES if layer == 0 else 0)
                v.wait_ge(g["loaded"], 64 * k + 64)
                link(nc.vector.tensor_copy(e_dstf[:], e_dst[:]))
                link(nc.vector.tensor_scalar(same, dst_row, e_dstf[:], None, ALU.is_equal))
                link(nc.vector.tensor_tensor(earlier, same, before, ALU.mult))
                link(nc.vector.tensor_reduce(e_flag[:], earlier, AX.X, ALU.max))
                link(nc.vector.scalar_tensor_tensor(e_flag[:], e_dstf[:], 0.0, e_flag[:], ALU.is_lt, ALU.max))
                link(nc.vector.tensor_scalar(e_far[:], e_dstf[:], -1.0, spare[:], ALU.mult, ALU.add))
                nc.vector.scalar_tensor_tensor(e_to[:], e_far[:], e_flag[:], e_dstf[:], ALU.mult, ALU.add).then_inc(g["to"], 1)
                if layer == 0:
                    nc.vector.tensor_scalar(e_typ_oh, e_typ, rel_id[0:RELS, :], None, ALU.is_equal).then_inc(g["types"], 1)
                    v.wait_ge(g["products"], k + 1)
                    link(nc.vector.tensor_scalar(e_coef[:], bank[3][:, 0:BASES], norm[:, bass.ds(k, 1)], None, ALU.mult))
                    for b in range(BASES):
                        product = bank[1 + b // 4][:, (b % 4) * FEAT:(b % 4 + 1) * FEAT]
                        if b == 0:
                            link(nc.vector.tensor_scalar(message[:, 0:FEAT], product, e_coef[:, 0:1], None, ALU.mult))
                        else:
                            link(nc.vector.scalar_tensor_tensor(message[:, 0:FEAT], product, e_coef[:, b:b + 1],
                                                                message[:, 0:FEAT], ALU.mult, ALU.add))
                    nc.vector.tensor_scalar(message[:, FEAT:FEAT + 1], e_dstf[:], 0.0, None,
                                            ALU.is_ge).then_inc(g["message"], 1)
                assert n[0] == steps
                v.wait_ge(g["summed"], k + 1)
                v.wait_ge(g["to"], k + 1)
                nc.vector.tensor_copy(total[:, 0:width], bank[4][:, 0:width]).then_inc(g["total"], 1)
            for t, r in tiles:
                v.wait_ge(g["back_turned"], t + 1)
                to, ps = acc[:, t * P:t * P + r], bank[t % 2][:, 0:r]
                if layer == 0:
                    nc.vector.tensor_scalar(to, ps, bias0_col[:], None, ALU.add).then_inc(g["back_added"], 1)
                    v.wait_ge(g["back"], 16 * t + 16)
                    nc.vector.tensor_scalar(deg[0:r, t:t + 1], total[0:r, FEAT:FEAT + 1], 1.0, None,
                                            ALU.add).then_inc(g["back_taken"], 1)
                else:
                    nc.vector.tensor_scalar(to, ps, 1.0 / ZSCALE, None, ALU.mult).then_inc(g["back_added"], 1)
                    nc.vector.engine_nop().then_inc(g["back_taken"], 1)
            v.wait_ge(g["back_added"], TILES)

        def general_tensor(pe, layer):
            g = general[layer]
            width = FEAT + 1 - layer
            with pe.Fori(0, CHUNKS) as k:
                pe.wait_ge(g["gathered"], 16 * k + 16)
                if layer == 0:
                    nc.tensor.transpose(bank[0][:, 0:P], e_rows, ident[:]).then_inc(g["turned"], 1)
                    pe.wait_ge(g["types"], k + 1)
                    at = (Q - 1) * Q * BASES
                    nc.tensor.matmul(bank[3][:, 0:BASES], e_typ_oh, wcomp_bd[0:RELS, at:at + BASES], start=True, stop=True)
                    pe.wait_ge(g["xt"], k + 1)
                    for half in range(2):
                        last = nc.tensor.matmul(bank[1 + half][:], e_xt,
                                                wt[:, 4 * half:4 * half + 4, :].rearrange("p b f -> p (b f)"),
                                                start=True, stop=True)
                    last.then_inc(g["products"], 1)
                    pe.wait_ge(g["message"], k + 1)
                else:
                    pe.wait_ge(g["to"], k + 1)
                nc.tensor.matmul(bank[4][:, 0:width], same, message[:, 0:width], start=True, stop=True).then_inc(g["summed"], 1)
            for t, r in tiles:
                pe.wait_ge(g["back"], 16 * t + 16)
                if t >= 2:
                    pe.wait_ge(g["back_added"], t - 1)
                last = nc.tensor.matmul(bank[t % 2][:, 0:r], total[0:r, 0:FEAT], ident[0:r, 0:r], start=True,
                                        stop=(layer == 1))
                if layer == 0:
                    last = nc.tensor.matmul(bank[t % 2][:, 0:r], loop_sb[:], xt[:, t * P:t * P + r], start=False, stop=True)
                last.then_inc(g["back_turned"], 1)

        @block.sync
        def _(sp):
            def load_idx(i, h):
                sp.dma_start(idx[:, h, :], src_idx[bass.ds(i, 1), h].rearrange("o p k -> (o p) k")).then_inc(idx_loaded[h], 16)

            def load_types(i):
                for q in range(Q):
                    sp.dma_start(typ[RELS * q:RELS * (q + 1), :, :].rearrange("p a b -> p (a b)"),
                                 types[bass.ds(i, 1), q].rearrange("o u n -> (o u) n").broadcast_to([RELS, Q * P])).then_inc(typ_loaded, 16)
            sp.dma_start(idx[:, 0, :], src_idx[0, 0]).then_inc(idx_loaded[0], 16)
            sp.dma_start(src_i, src_t).then_inc(ld_edges, 16)
            sp.dma_start(dst_i, dst_t).then_inc(ld_edges, 16)
            sp.dma_start(start_b, starts[:, LEAD:LEAD + CHUNKS].broadcast_to([P, CHUNKS])).then_inc(ld_edges, 16)
            sp.wait_ge(tail_zero, 1)
            for part, (a, b) in enumerate(x_parts):
                sp.dma_start(x_nm[:, a:b, :], x[a * P:b * P, :].rearrange("(t p) f -> p t f", p=P)).then_inc(ld_x[part], 16)
            sp.dma_start(x_nm[0:LAST, full, :], x[full * P:NODES, :]).then_inc(ld_x[-1], 16)
            sp.dma_start(idx[:, 1, :], src_idx[0, 1]).then_inc(idx_loaded[1], 16)
            load_types(0)
            sp.dma_start(start_i[:], starts).then_inc(ld_norm, 16)
            sp.dma_start(norm[:, 0:CHUNKS], norm_t).then_inc(ld_norm, 16)
            sp.dma_start(loop_sb[:], loop_w).then_inc(ld_loop, 16)
            sp.dma_start(bias0_col[:], bias0.rearrange("(f o) -> f o", o=1)).then_inc(ld_loop, 16)
            sp.wait_ge(wbd_zero, 1)
            for q in range(Q):
                sp.dma_start(wcomp_bd[RELS * q:RELS * (q + 1), (Q - 1) * Q * BASES + BASES * q:(Q - 1) * Q * BASES + BASES * (q + 1)], w_comp).then_inc(ld_w, 16)
            sp.dma_start(wt[:], weight.rearrange("b d f -> d b f")).then_inc(ld_w, 16)
            sp.dma_start(w1_sb[:], w1).then_inc(ld_w, 16)
            sp.dma_start(bias1_b[:], bias1.rearrange("(o f) -> o f", o=1).broadcast_to([P, FEAT])).then_inc(ld_w, 16)
            narrow = is_narrow(sp)
            with sp.Fori(0, STEPS) as i:
                sp.wait_ge(typ_done, i + 1)
                load_types(i + 1)
                for h in range(2):
                    for j in range(GROUP * h, GROUP * h + GROUP):
                        sp.wait_ge(gathered[j], 16 * i + 16)
                    load_idx(i + 1, h)
            with sp.If(narrow):
                sp.wait_ge(flag_ready, 1)
            with sp.Else():
                general_sync(sp, 0)
                general_sync(sp, 1)
            for n, quad in enumerate(quads):
                sp.wait_ge(out_ready, n + 1)
                whole = [t for t, r in quad if r == P]
                a, b = whole[0], whole[-1] + 1
                sp.dma_start(out[a * P:b * P, :].rearrange("(t p) f -> p t f", p=P), x_nm[:, a:b, :]).then_inc(stored, 16)
            sp.dma_start(out[full * P:NODES, :], x_nm[0:LAST, full, :]).then_inc(stored, 16)
            sp.wait_ge(stored, 16 * (len(quads) + 1))

        @block.gpsimd
        def _(pool):
            def gather(j):
                return pool.indirect_dma_start(
                    rows[:, j, :], None, x[:, :],
                    bass.IndirectOffsetOnAxis(ap=idx[:, j // GROUP, j % GROUP:j % GROUP + 1], axis=0)).then_inc(gathered[j], 16)

            nc.gpsimd.iota(lane_i[:], [[0, 1]], base=0, channel_multiplier=1)
            nc.gpsimd.iota(iota_lo[:], [[1, P]], base=0, channel_multiplier=0, allow_small_or_imprecise_dtypes=True)
            nc.gpsimd.iota(iota_key[:], [[1, KEYS]], base=0, channel_multiplier=0, allow_small_or_imprecise_dtypes=True).then_inc(iotas, 1)
            nc.gpsimd.memset(ident[:], 1.0).then_inc(iotas, 1)
            pool.wait_ge(iotas, 2)
            nc.gpsimd.affine_select(out=ident[:], in_=ident[:], compare_op=ALU.is_equal, fill=0.0, base=0,
                                    pattern=[[-1, P]], channel_multiplier=1).then_inc(iotas, 1)
            for h in range(2):
                pool.wait_ge(idx_loaded[h], 16)
                for j in range(GROUP * h, GROUP * h + GROUP):
                    gather(j)
                if h == 0:
                    nc.gpsimd.memset(g_sb[:], 0.0).then_inc(g_taken, 4)
                    nc.gpsimd.memset(count_words[:, 0:ZERO_POOL], 0).then_inc(zeroed, 1)
            narrow = is_narrow(pool)
            with pool.Fori(1, STEPS) as i:
                for h in range(2):
                    pool.wait_ge(idx_loaded[h], 16 * i + 16)
                    for j in range(GROUP * h, GROUP * h + GROUP):
                        pool.wait_ge(cnt_ready, STEP * i - STEP + j + 1 + LAG)
                        pool.sem_inc(slot_free, 1)
                        gather(j)

            def add_bias():
                pool.wait_ge(ld_w, 16 * (Q + 3))
                for n, quad in enumerate(quads):
                    t0, k = quad[0][0], len(quad)
                    pool.wait_ge(h_ready, n + 1)
                    nc.gpsimd.tensor_tensor(h_nm[:, t0:t0 + k], h_nm[:, t0:t0 + k],
                                            bias1_b[:].unsqueeze(1).broadcast_to([P, k, FEAT]), ALU.add).then_inc(res_ready, 1)

            with pool.If(narrow):
                for n, quad in enumerate(quads):
                    t0, k = quad[0][0], len(quad)
                    pool.wait_ge(zhi_ready, n + 1)
                    nc.gpsimd.tensor_tensor(z_lo[:, t0:t0 + k], z_f[:, t0:t0 + k], z_hi[:, t0:t0 + k],
                                            ALU.subtract).then_inc(zlo_ready, 1)
                add_bias()
            with pool.Else():
                general_gpsimd(pool, 0)
                add_bias()
                general_gpsimd(pool, 1)

        @block.scalar
        def _(act):
            def deviation(to, n, ready, done):
                t0, k = quads[n][0][0], len(quads[n])
                act.wait_ge(ready, n + 1)
                nc.scalar.activation(to[:, t0:t0 + k], mv[:, t0:t0 + k, 1], ACT.Sqrt, bias=eps_col[:]).then_inc(done, 1)

            def one_hot_lo(g, h, n):
                if not isinstance(n, int):
                    act.wait_ge(lo_ready, n - 1)
                for j in range(GROUP):
                    last = nc.scalar.activation(lo_abs[:, j, :], iota_lo[:], ACT.Abs, bias=neg_lo[:, bass.ds(GROUP * g + j, 1)])
                last.then_inc(lo_step, 1)
                act.wait_ge(lo_step, n)
                nc.scalar.activation(lo_oh[:, h], lo_abs[:], ACT.Relu, bias=1.0, scale=-1.0).then_inc(lo_ready, 1)

            act.wait_ge(zero_ready, 1)
            nc.scalar.activation(count_words[:, ZERO_POOL:ZERO_POOL + ZERO_ACT], zero_col[:].broadcast_to([P, ZERO_ACT]),
                                 ACT.Copy).then_inc(zeroed, 1)
            act.wait_ge(iotas, 1)
            act.wait_ge(nums_ready, 1)
            one_hot_lo(0, 0, 1)

            def loop_bias(n):
                a, width = blocks[n]
                act.wait_ge(init_ready, n + 1)
                nc.scalar.activation(acc[:, a:a + width], bank[2 + n % 2][:, 0:width], ACT.Identity,
                                     bias=bias0_col[:]).then_inc(init_taken, 1)

            act.wait_ge(ld_loop, 32)
            for n, (a, width) in enumerate(blocks):
                act.wait_ge(xt_ready, n + 1)
                nc.scalar.copy(xt[:, a:a + width], bank[n % 2][:, 0:width]).then_inc(xt_taken, 1)
                if n:
                    loop_bias(n - 1)
            act.wait_ge(coef_ready, 1)
            nc.scalar.copy(coef_raw[:], coef_ps[:]).then_inc(coef_copied, 1)
            loop_bias(len(blocks) - 1)
            act.wait_ge(coef_copied, 1)
            narrow = is_narrow(act)
            with act.Fori(0, STEPS) as i:
                for h in range(2):
                    g = 2 * i + h
                    act.wait_ge(cnt_ready, GROUP * g + LAG)
                    one_hot_lo(g + 1, 1 - h, g + 2)
                    act.wait_ge(z_ready, g + 1)
                    for q in range(2):
                        act.wait_ge(g_ready, 2 * g + q + 1)
                        if h == 0 and q == 1:
                            act.wait_ge(coef_taken, i + 1)
                            nc.scalar.copy(coef_raw[:], coef_ps[:]).then_inc(coef_copied, 1)
                        nc.scalar.copy(g_sb[:, h].rearrange("p b (c n) -> p c b n", n=WIN)[:, 4 * q:4 * q + 4],
                                       g_ps[q][:, 0:4 * BASES * WIN].rearrange("p (c b n) -> p c b n", b=BASES, n=WIN)
                                       ).then_inc(g_taken, 1)

            def convert(n):
                a, width = blocks[n]
                if n >= 2:
                    act.wait_ge(agg_ready, n - 1)
                nc.scalar.copy(cnt16[:, n % 2, 0:ACT_ROWS, 0:width], count[:, 0:ACT_ROWS, a:a + width]).then_inc(cv_act, 1)

            def first_end(fast):
                act.wait_ge(sums_ready, 1 if fast else 2)
                nc.scalar.activation(dinv[:], deg[:], ACT.Sqrt).then_inc(dinv_sqrt, 1)

                def z_part(n):
                    quad = quads[n]
                    t0, k = quad[0][0], len(quad)
                    act.wait_ge(scale_ready, n + 1)
                    for t, _ in quad:
                        last = nc.scalar.activation(z_f[:, t, :], x_nm[:, t, :], ACT.Identity, bias=shift_z[:, t:t + 1],
                                                    scale=scale_z[:, t:t + 1])
                    last.then_inc(zf_ready, 1)
                    if fast:
                        act.wait_ge(zf_ready, n + 1)
                        nc.scalar.copy(z_hi[:, t0:t0 + k], z_f[:, t0:t0 + k]).then_inc(zhi_ready, 1)

                for n in range(len(quads)):
                    deviation(sdev, n, var_ready, sd_ready)
                    if n:
                        z_part(n - 1)
                z_part(len(quads) - 1)

            with act.If(narrow):
                act.wait_ge(z_ready, 2 * STEPS + 2)
                act.wait_ge(counts_added, CHUNKS + LAG + 2)
                nc.scalar.copy(cnt16[:, 0, 0:FIRST_ROWS, :], count[:, 0:FIRST_ROWS, 0:BLOCK]).then_inc(cv_first, 1)
                first_end(True)
                convert(1)
                for n, (a, width) in enumerate(blocks):
                    act.wait_ge(agg_ready, n + 1)
                    nc.scalar.activation(acc[:, a:a + width], bank[4 + n % 2][:, 0:width], ACT.Copy,
                                         scale=1.0 / ZSCALE).then_inc(agg_done, 1)
                    if n + 2 < len(blocks):
                        convert(n + 2)
                    deviation(sdev, n, var1, sd1)
            with act.Else():
                general_scalar(act, 0)
                first_end(False)
                for n in range(len(blocks)):
                    deviation(sdev, n, var1, sd1)

        @block.vector
        def _(v):
            nd = [0]

            def chain(ins):
                nd[0] += 1
                ins.then_inc(dve, 1)
                v.wait_ge(dve, nd[0])

            nc.vector.memset(x_nm[:, full, :], 0.0).then_inc(tail_zero, 1)
            nc.vector.memset(zero_col[:], 0.0).then_inc(zero_ready, 1)
            nc.vector.memset(wcomp_bd[:], 0.0).then_inc(wbd_zero, 1)
            nc.vector.memset(eps_col[:], EPS)
            nc.vector.memset(ones16[:], 1.0)
            nc.vector.memset(ones32[:], 1.0)
            for padded in (neg_lo, rel, norm):
                nc.vector.memset(padded[:, CHUNKS:], 0.0)
            nc.vector.memset(deg[:], 1.0)
            nc.vector.memset(mv[:], 1.0)
            nc.vector.memset(acc[:, NODES:], 0.0).then_inc(rows_added, 1)
            split = ZERO_POOL + ZERO_ACT
            nc.vector.memset(count_words[:, split:split + ZERO_DVE], 0.0)
            v.wait_ge(iotas, 1)
            chain(nc.vector.tensor_scalar(rel_id_i[:], lane_i[:], RELS - 1, None, ALU.bitwise_and))
            nc.vector.tensor_copy(lane[:], lane_i[:])
            nc.vector.tensor_copy(rel_id[:], rel_id_i[:])
            v.wait_ge(ld_edges, 48)
            chain(nc.vector.tensor_scalar(work_i, src_i, P - 1, None, ALU.bitwise_and))
            nc.vector.tensor_scalar(neg_lo[:, 0:CHUNKS], work_i, -1.0, None, ALU.mult).then_inc(nums_ready, 1)
            v.wait_ge(nums_ready, 1)
            chain(nc.vector.tensor_tensor(rel[:, 0:CHUNKS], dst_i, start_b, ALU.subtract))
            chain(nc.vector.tensor_scalar(work_i, src_i, 7, None, ALU.logical_shift_right))
            chain(nc.vector.scalar_tensor_tensor(key[:], work_i, float(WIN), rel[:, 0:CHUNKS], ALU.mult, ALU.add))

            def type_one_hot(i):
                v.wait_ge(typ_loaded, 64 * i + 64)
                nc.vector.tensor_scalar(typ_oh[:], typ[:], rel_id[:], None, ALU.is_equal).then_inc(typ_done, 1)

            type_one_hot(0)
            nc.vector.memset(count_words[:, split + ZERO_DVE:], 0.0).then_inc(counts_added, 1)
            v.wait_ge(counts_added, 1)
            v.wait_ge(zeroed, 2)
            v.wait_ge(iotas, 3)
            squares = count[:].rearrange("p r n -> p (r n)")[:, 0:full * (NPAD + P)].rearrange("p (t w) -> p t w", t=full)
            nc.vector.tensor_copy(squares[:, :, 0:P], ident[:].unsqueeze(1).broadcast_to([P, full, P]))
            nc.vector.tensor_copy(count[:, full, full * P:NODES], ident[:, 0:LAST]).then_inc(counts_added, 1)
            v.wait_ge(counts_added, 2)
            n = CHUNKS - 1
            over = h_nm[:].rearrange("p t f -> p (t f)")[:, 4 * CHUNKS:5 * CHUNKS]
            nc.vector.tensor_scalar(least[:], lane[:], P - 1, None, ALU.is_equal)
            nc.vector.tensor_scalar(spare[:], lane[:], float(NODES), None, ALU.add)
            nc.vector.tensor_reduce(tests[:, 0:1], rel[:, 0:CHUNKS], AX.X, ALU.max)
            nc.vector.tensor_reduce(tests[:, 1:2], rel[:, 0:n], AX.X, ALU.min)
            nc.vector.tensor_tensor(over[:, 0:n], dst_i[:, 0:n], start_b[:, 1:CHUNKS], ALU.subtract)
            chain(nc.vector.tensor_scalar(tests[:, 3:4], dst_i[:, n:CHUNKS], 0.0, None, ALU.is_ge))
            nc.vector.scalar_tensor_tensor(tests[:, 3:4], rel[:, n:CHUNKS], 0.0, tests[:, 3:4], ALU.is_lt, ALU.mult)
            nc.vector.tensor_reduce(tests[:, 2:3], over[:, 0:n], AX.X, ALU.max)
            nc.vector.tensor_scalar(tests[:, 0:1], tests[:, 0:1], float(WIN), None, ALU.is_ge)
            chain(nc.vector.tensor_scalar(tests[:, 1:2], tests[:, 1:2], least[:], None, ALU.is_lt))
            chain(nc.vector.tensor_scalar(tests[:, 2:3], tests[:, 2:3], 0.0, None, ALU.is_gt))
            nc.vector.tensor_reduce(bad[:], tests[:], AX.X, ALU.max).then_inc(bad_ready, 1)
            v.wait_ge(ld_norm, 32)

            def add_counts(start, c, j, n):
                v.wait_ge(cnt_ready, c)
                v.wait_ge(counts_added, n)
                w = count[:, :, bass.ds(start, WIN)]
                nc.vector.tensor_tensor(w, w, cnt_ps[j % 4][:, 0:ROWS * WIN].rearrange("p (r n) -> p r n", n=WIN),
                                        ALU.add).then_inc(counts_added, 1)

            def add_rows(start, h, k, n):
                v.wait_ge(rows_added, n)
                w = acc[:, bass.ds(start, WIN)]
                nc.vector.tensor_tensor(w, w, z_ps[h][:, k * WIN:(k + 1) * WIN], ALU.add).then_inc(rows_added, 1)

            def load_starts(at, n):
                _, vals = nc.values_load_multi_w_load_instructions(
                    start_i[0:1, bass.ds(at, n)], engines=[mybir.EngineType.DVE], min_val=0, max_val=NODES - 1,
                    skip_runtime_bounds_check_because="window starts are destination nodes, below 3125")
                return vals

            def coefficients(i):
                v.wait_ge(coef_copied, i + 1)
                nc.vector.tensor_tensor(
                    coef[:].rearrange("p (q j) b -> p q j b", q=Q),
                    coef_raw[:].rearrange("p (j q b) -> p q j b", q=Q, b=BASES),
                    norm[:, bass.ds(STEP * i, STEP)].rearrange("p (q j) -> p q j", q=Q).unsqueeze(3).broadcast_to([P, Q, Q, BASES]),
                    ALU.mult).then_inc(coef_taken, 1)

            def window_one_hot(g, h):
                nc.vector.tensor_tensor(
                    win_oh[:, h], iota_key[:, 0:WIN].unsqueeze(1).broadcast_to([P, GROUP, WIN]),
                    rel[:, bass.ds(GROUP * g, GROUP)].unsqueeze(2).broadcast_to([P, GROUP, WIN]),
                    ALU.is_equal).then_inc(win_ready, 1)

            def scatter(g, h, steps_taken):
                v.wait_ge(win_ready, g + 1)
                v.wait_ge(coef_taken, steps_taken)
                nc.vector.tensor_tensor(
                    scat[:, h], win_oh[:, h].unsqueeze(2).broadcast_to([P, GROUP, BASES, WIN]),
                    coef[:, GROUP * h:GROUP * (h + 1), :].unsqueeze(3).broadcast_to([P, GROUP, BASES, WIN]),
                    ALU.mult).then_inc(scat_ready, 1)

            coefficients(0)
            window_one_hot(0, 0)
            scatter(0, 0, 1)
            v.wait_ge(bad_summed, 1)
            nc.vector.tensor_scalar(flag[:], bank[4][0:1, 0:1], 1.0, None, ALU.min).then_inc(flag_ready, 1)
            narrow = is_narrow(v)
            v.wait_ge(init_taken, len(blocks))
            with v.Fori(0, STEPS) as i:
                for h in range(2):
                    g = 2 * i + h
                    a_start = load_starts(GROUP * g, GROUP)
                    c_start = load_starts(GROUP * g + LEAD - LAG, GROUP)
                    for j in range(GROUP):
                        c = GROUP * g + j
                        nc.vector.tensor_scalar(key_oh[:, h, j, 0:KEYS], iota_key[:], key[:, bass.ds(c, 1)], None,
                                                ALU.is_equal).then_inc(key_ready, 1)
                        if j == 0:
                            v.wait_ge(z_ready, g + 1)
                        add_rows(a_start[j], h, j, c + 1)
                        add_counts(c_start[j], c + 1, j - LAG, c + 2)
                        if j == 0 and h == 0:
                            type_one_hot(i + 1)
                        if j == 3 and h == 1:
                            coefficients(i + 1)
                        if j == 3:
                            window_one_hot(g + 1, 1 - h)
                        if j == 4:
                            scatter(g + 1, 1 - h, i + 1 + h)

            def last_sums():
                c_start = load_starts(CHUNKS + LEAD - LAG, LAG)
                for k in range(LAG):
                    add_counts(c_start[k], CHUNKS + k + 1, k - LAG, CHUNKS + k + 2)
                n = CHUNKS + 1
                part = NPAD // GROUP
                for g in (2 * STEPS, 2 * STEPS + 1):
                    a_start = load_starts(GROUP * g, GROUP)
                    v.wait_ge(z_ready, g + 1)
                    for k in range(GROUP):
                        add_rows(a_start[k], g % 2, k, n)
                        n += 1
                        if g == 2 * STEPS:
                            if k == 0:
                                v.wait_ge(counts_added, CHUNKS + LAG + 2)
                            ins = nc.vector.tensor_copy(deg_part[:, part * k:part * (k + 1)],
                                                        count[:, TILES, part * k:part * (k + 1)])
                            if k == GROUP - 1:
                                ins.then_inc(deg_ready, 1)
                        else:
                            row, half = TILES - FIRST_DVE + k // 2, BLOCK // 2 * (k % 2)
                            nc.vector.tensor_copy(cnt16[:, 0, row, half:half + BLOCK // 2],
                                                  count[:, row, half:half + BLOCK // 2])
                assert part * GROUP == NPAD and 2 * FIRST_DVE == GROUP
                v.wait_ge(degt_ready, 1)
                nc.vector.tensor_scalar(deg[:, 0:full], bank[1][:, 0:full], 1.0, None, ALU.add)
                nc.vector.tensor_scalar(deg[0:LAST, full:TILES], bank[1][0:LAST, full:TILES], 1.0, None,
                                        ALU.add).then_inc(sums_ready, 1)

            links = [0]

            def link(ins):
                links[0] += 1
                ins.then_inc(tail, 1)
                v.wait_ge(tail, links[0])

            def flat(ap):
                return ap.rearrange("p a b -> p (a b)")

            def first_end():
                def numbers(n):
                    t0, k = quads[n][0][0], len(quads[n])
                    to = slice(t0, t0 + k)
                    v.wait_ge(sd_ready, n + 1)
                    link(nc.vector.reciprocal(rstd[:, to], sdev[:, to]))
                    link(nc.vector.scalar_tensor_tensor(scale_z[:, to], rstd[:, to], ZSCALE, dinv[:, to], ALU.mult, ALU.mult))
                    nc.vector.scalar_tensor_tensor(shift_z[:, to], mv[:, to, 0], -1.0, scale_z[:, to],
                                                   ALU.mult, ALU.mult).then_inc(scale_ready, 1)

                for n, quad in enumerate(quads):
                    v.wait_ge(t_ready, n + 1)
                    t0, k, r = quad[0][0], len(quad), quad[0][1]
                    whole = [q for q in quad if q[1] == P]
                    for a, m, r in ((t0, len(whole), P), (full, k - len(whole), LAST)):
                        if m:
                            ins = nc.vector.scalar_tensor_tensor(
                                flat(x_nm[0:r, a:a + m, :]), bank[n % 4][0:r, (a - t0) * FEAT:(a - t0 + m) * FEAT], 0.0,
                                flat(x_nm[0:r, a:a + m, :]), ALU.max, ALU.add)
                    ins.then_inc(t_taken, 1)
                    v.wait_ge(t_taken, n + 1)
                    for t, r in quad:
                        ins = nc.vector.bn_stats(stats[0:r, t, :], x_nm[0:r, t, :])
                    link(ins)
                    for t, r in quad:
                        ins = nc.vector.bn_aggr(mv[0:r, t, :], stats[0:r, t, :])
                    ins.then_inc(var_ready, 1)
                    if n == 0:
                        v.wait_ge(dinv_sqrt, 1)
                        link(nc.vector.reciprocal(dinv[:], dinv[:]))
                    else:
                        numbers(n - 1)
                numbers(len(quads) - 1)

            def residual():
                for n, quad in enumerate(quads):
                    for t, r in quad:
                        ins = nc.vector.tensor_scalar(h_nm[:, t, :], x_nm[:, t, :], mv[:, t, 0:1], rstd[:, t:t + 1],
                                                      ALU.subtract, ALU.mult)
                    ins.then_inc(h_ready, 1)

            def convert(n):
                a, width = blocks[n]
                if n >= 2:
                    v.wait_ge(agg_ready, n - 1)
                nc.vector.tensor_copy(cnt16[:, n % 2, ACT_ROWS:TILES, 0:width],
                                      count[:, ACT_ROWS:TILES, a:a + width]).then_inc(cv_dve, 1)

            def finish(n):
                quad = quads[n]
                t0, k = quad[0][0], len(quad)
                v.wait_ge(res_ready, n + 1)
                v.wait_ge(fin_ready, n + 1)
                for t, r in quad:
                    ins = nc.vector.scalar_tensor_tensor(
                        h_nm[0:r, t, :], bank[6 + n % 2][0:r, (t - t0) * FEAT:(t - t0 + 1) * FEAT], dinv[0:r, t:t + 1],
                        h_nm[0:r, t, :], ALU.mult, ALU.add)
                ins.then_inc(fin_taken, 1)
                v.wait_ge(fin_taken, n + 1)
                for t, r in quad:
                    ins = nc.vector.bn_stats(stats[0:r, t, :], h_nm[0:r, t, :])
                link(ins)
                for t, r in quad:
                    ins = nc.vector.bn_aggr(mv[0:r, t, :], stats[0:r, t, :])
                ins.then_inc(var1, 1)
                v.wait_ge(sd1, n + 1)
                link(nc.vector.reciprocal(rstd[:, t0:t0 + k], sdev[:, t0:t0 + k]))
                for t, r in quad:
                    ins = nc.vector.tensor_scalar(x_nm[0:r, t, :], h_nm[0:r, t, :], mv[0:r, t, 0:1], rstd[0:r, t:t + 1],
                                                  ALU.subtract, ALU.mult)
                ins.then_inc(out_ready, 1)

            last_sums()
            with v.If(narrow):
                first_end()
                nc.vector.tensor_copy(cnt16[:, 0, FIRST_ROWS:TILES - FIRST_DVE, :],
                                      count[:, FIRST_ROWS:TILES - FIRST_DVE, 0:BLOCK]).then_inc(cv_first_dve, 1)
                convert(1)
                residual()
                for n in range(len(blocks)):
                    if n + 2 < len(blocks):
                        convert(n + 2)
                    finish(n)
            with v.Else():
                links[0] = 0
                general_vector(v, 0)
                nc.vector.engine_nop().then_inc(sums_ready, 1)
                first_end()
                residual()
                general_vector(v, 1)
                nc.vector.engine_nop().then_inc(agg_done, len(blocks))
                for n in range(len(blocks)):
                    finish(n)

        @block.tensor
        def _(pe):
            pe.wait_ge(iotas, 3)

            def turn_x(n):
                if n % 2 == 0:
                    pe.wait_ge(ld_x[n // 2], 16)
                if n == len(quads) - 1:
                    pe.wait_ge(tail_zero, 1)
                if n >= 2:
                    pe.wait_ge(xt_taken, n - 1)
                for t, r in quads[n]:
                    c = (t - quads[n][0][0]) * P
                    last = nc.tensor.transpose(bank[n % 2][:, c:c + r], x_nm[0:r, t, :], ident[0:r, 0:r])
                last.then_inc(xt_ready, 1)

            def loop_product(n):
                a, width = blocks[n]
                pe.wait_ge(xt_taken, n + 1)
                if n >= 2:
                    pe.wait_ge(init_taken, n - 1)
                nc.tensor.matmul(bank[2 + n % 2][:, 0:width], loop_sb[:], xt[:, a:a + width],
                                 start=True, stop=True).then_inc(init_ready, 1)

            turn_x(0)
            pe.wait_ge(ld_loop, 32)
            for n in range(1, len(quads)):
                turn_x(n)
                loop_product(n - 1)

            def second_product(h, b):
                last = nc.tensor.matmul(z_ps[h][:, 0:GROUP * WIN], wt[:, b, :], g_sb[:, h, b, :],
                                        start=(b == 0), stop=(b == BASES - 1))
                if b == BASES - 1:
                    last.then_inc(z_ready, 1)

            def look_up(i):
                pe.wait_ge(typ_done, i + 1)
                for j in range(Q):
                    at = (Q - 1 - j) * Q * BASES
                    last = nc.tensor.matmul(coef_ps[:], typ_oh[:, j, :], wcomp_bd[:, at:at + Q * Q * BASES],
                                            start=(j == 0), stop=(j == Q - 1))
                return last

            pe.wait_ge(ld_w, 16 * (Q + 3))
            look_up(0).then_inc(coef_ready, 1)
            loop_product(len(quads) - 1)
            pe.wait_ge(bad_ready, 1)
            nc.tensor.matmul(bank[4][0:1, 0:1], bad[:], ones32[:], start=True, stop=True).then_inc(bad_summed, 1)
            pe.wait_ge(coef_copied, 1)
            pe.wait_ge(g_taken, 4)
            for b in range(BASES):
                second_product(0, b)
            narrow = is_narrow(pe)
            pe.wait_ge(init_taken, len(blocks))
            zeros = g_sb[:, 0].rearrange("p b n -> p (b n)")
            for k in range(LAG):
                nc.tensor.matmul(cnt_ps[4 - LAG + k][:, 0:ROWS * WIN], zeros[:, 0:P], zeros[:, 0:ROWS * WIN],
                                 start=True, stop=True).then_inc(cnt_ready, 1)
            with pe.Fori(0, STEPS) as i:
                for h in range(2):
                    g = 2 * i + h
                    for j in range(GROUP):
                        q, jj, c = j // 4, j % 4, GROUP * g + j
                        if j == 0:
                            pe.wait_ge(scat_ready, g + 1)
                        if jj == 0:
                            pe.wait_ge(g_taken, 2 * g + q + 3)
                        if j == 4 and h == 0:
                            look_up(i + 1)
                        pe.wait_ge(gathered[GROUP * h + j], 16 * i + 16)
                        last = nc.tensor.matmul(g_ps[q][:, jj * BASES * WIN:(jj + 1) * BASES * WIN],
                                                rows[:, GROUP * h + j, :],
                                                scat[:, h, j].rearrange("p b n -> p (b n)"), start=True, stop=True)
                        if jj == 3:
                            last.then_inc(g_ready, 1)
                        if j == 1:
                            pe.wait_ge(g_taken, 2 * g + 4)
                            pe.wait_ge(rows_added, GROUP * g + 1)
                        for b in range(BASES)[max(j - 1, 0):j + j // (GROUP - 1)]:
                            second_product(1 - h, b)
                        pe.wait_ge(key_ready, c + 1)
                        if j == 0:
                            pe.wait_ge(lo_ready, g + 1)
                        pe.wait_ge(counts_added, c + 1)
                        nc.tensor.matmul(cnt_ps[j % 4][:, 0:KEYS + WIN], lo_oh[:, h, j, :], key_oh[:, h, j, :],
                                         start=True, stop=True).then_inc(cnt_ready, 1)

            def first_end(fast):
                for n, quad in enumerate(quads):
                    if n >= 4:
                        pe.wait_ge(t_taken, n - 3)
                    for t, r in quad:
                        c = (t - quad[0][0]) * P
                        last = nc.tensor.transpose(bank[n % 4][0:r, c:c + P], acc[:, t * P:t * P + r], ident[:])
                    last.then_inc(t_ready, 1)
                if fast:
                    for n in range(len(quads)):
                        first_block(n)

            def pair_products(n, t):
                width = blocks[n][1]
                for half in (z_hi, z_lo):
                    last = nc.tensor.matmul(bank[4 + n % 2][:, 0:width], half[:, t, :], cnt16[:, n % 2, t, 0:width],
                                            start=(t == 0 and half is z_hi), stop=(t == TILES - 1 and half is z_lo))
                return last

            def first_block(q):
                pe.wait_ge(zlo_ready, q + 1)
                for t, _ in quads[q]:
                    if t == 0:
                        pe.wait_ge(cv_first, 1)
                    elif t == FIRST_ROWS:
                        pe.wait_ge(cv_first_dve, 1)
                    last = pair_products(0, t)
                if q == len(quads) - 1:
                    last.then_inc(agg_ready, 1)

            def project(n):
                pe.wait_ge(agg_done, n + 1)
                if n >= 2:
                    pe.wait_ge(fin_taken, n - 1)
                for t, r in quads[n]:
                    c = (t - quads[n][0][0]) * FEAT
                    last = nc.tensor.matmul(bank[6 + n % 2][0:r, c:c + FEAT], acc[:, t * P:t * P + r], w1_sb[:],
                                            start=True, stop=True)
                last.then_inc(fin_ready, 1)

            pe.wait_ge(g_taken, 4 * STEPS + 4)
            pe.wait_ge(rows_added, CHUNKS + 1)
            for b in range(BASES):
                second_product(1, b)
            pe.wait_ge(deg_ready, 1)
            for t, r in tiles:
                last = nc.tensor.matmul(bank[1][0:r, t:t + 1], deg_part[:, t * P:t * P + r], ones16[:, 0:1],
                                        start=True, stop=True)
            last.then_inc(degt_ready, 1)
            pe.wait_ge(sums_ready, 1)
            with pe.If(narrow):
                first_end(True)
                for n in range(1, len(blocks)):
                    pe.wait_ge(cv_act, n)
                    pe.wait_ge(cv_dve, n)
                    if n >= 2:
                        pe.wait_ge(agg_done, n - 1)
                    for t in range(TILES):
                        last = pair_products(n, t)
                        if t == TILES // 2:
                            project(n - 1)
                    last.then_inc(agg_ready, 1)
                project(len(blocks) - 1)
            with pe.Else():
                general_tensor(pe, 0)
                pe.wait_ge(sums_ready, 2)
                first_end(False)
                general_tensor(pe, 1)
                for n in range(len(blocks)):
                    project(n)


def kernel(x, src, dst, edge_type_32, edge_weight1, L0_gnn_weight, L0_gnn_w_comp, L0_gnn_loop_weight,
           L0_gnn_h_bias, L1_gnn_W, L1_gnn_b):
    import numpy as np
    import concourse.bacc as bacc
    from concourse.bass_utils import run_bass_kernel_spmd

    def arr(a):
        return np.ascontiguousarray(a)

    pad = CHUNKS * P - EDGES
    src, dst, types = (np.asarray(a) for a in (src, dst, edge_type_32))
    src_p = np.pad(src, (0, pad)).reshape(CHUNKS, P)
    dst_p = np.pad(dst, (0, pad), constant_values=-1).reshape(CHUNKS, P)
    norm_p = np.pad(np.asarray(edge_weight1)[:, 0], (0, pad)).reshape(CHUNKS, P)
    step = STEP * P
    arrays = {
        "x": arr(x),
        "src_idx": arr(np.pad(src_p, ((0, STEP), (0, 0))).reshape(STEPS + 1, 2, GROUP, P).transpose(0, 1, 3, 2)),
        "src_t": arr(src_p.T), "dst_t": arr(dst_p.T), "src_rows": arr(src_p), "dst_rows": arr(dst_p),
        "starts": arr(np.pad(dst[::P], (LEAD, 0))[None]),
        "types": arr(np.pad(types, (0, pad + step)).reshape(STEPS + 1, Q, 1, Q * P)),
        "type_rows": arr(np.pad(types, (0, pad)).reshape(CHUNKS, P)),
        "norm_t": arr(norm_p.T),
        "weight": arr(L0_gnn_weight), "w_comp": arr(L0_gnn_w_comp), "loop_w": arr(L0_gnn_loop_weight),
        "bias0": arr(L0_gnn_h_bias), "w1": arr(L1_gnn_W), "bias1": arr(L1_gnn_b),
    }
    nc = bacc.Bacc("TRN2", target_bir_lowering=False, num_devices=1)
    args = [nc.dram_tensor(name, a.shape, mybir.dt.from_np(a.dtype), kind="ExternalInput").ap()
            for name, a in arrays.items()]
    out = nc.dram_tensor("out", (NODES, FEAT), F32, kind="ExternalOutput").ap()
    gnn_kernel(nc, *args, out)
    result = run_bass_kernel_spmd(nc, [arrays], core_ids=[0])
    return result.results[0]["out"]
```

```python
from contextlib import ExitStack

import concourse.bass as bass
import concourse.mybir as mybir

F32, F16, I32, U8 = mybir.dt.float32, mybir.dt.float16, mybir.dt.int32, mybir.dt.uint8
ALU = mybir.AluOpType
ACT = mybir.ActivationFunctionType
AX = mybir.AxisListType

P = 128
NODES, FEAT, EDGES, RELS, BASES = 3125, 128, 53125, 32, 8
CHUNKS = -(-EDGES // P)
GROUP = 8
STEP = 2 * GROUP
STEPS = CHUNKS // STEP
WIN = 12
TILES = -(-NODES // P)
LAST = NODES - (TILES - 1) * P
NPAD = 3136
KEYS = TILES * WIN
ROWS = TILES + 1
LEAD = STEP
LAG = 2
EPS = 1e-5
ACT_ROWS = (0, 11) + 5 * (14,)
FIRST_ROWS, FIRST_DVE = 15, 4
ZSCALE = 2048.0
ZERO_ACT, ZERO_DVE, ZERO_DMA, ZERO_DMAS = 5500, 6500, 2 * BASES * GROUP * WIN, 2
Q = P // RELS
BLOCK = 512


def gnn_kernel(nc, x, src_idx, src_t, dst_t, src_rows, dst_rows, starts, types, type_rows, norm_t, weight, w_comp,
               loop_w, bias0, w1, bias1, out):
    ctx = ExitStack()
    with ctx:
        def sb(name, shape, dt):
            return ctx.enter_context(nc.sbuf_tensor(name, shape, dt))

        def sem(name):
            return ctx.enter_context(nc.semaphore(name))

        cnt16 = sb("cnt16", [P, 2, TILES, BLOCK], F16)
        arena, used = cnt16[:].rearrange("p a b c -> p (a b c)"), [0]

        def carve(dims, dt, size):
            n = 1
            for d in dims:
                n *= d
            at, used[0] = used[0], used[0] + -(-n * size // 64) * 32
            assert used[0] <= 2 * TILES * BLOCK
            flat = arena[:, at:at + n * size // 2]
            flat = flat if dt == F16 else flat.bitcast(dt)
            names = "abcd"[:len(dims)]
            return flat.rearrange(f"p ({' '.join(names)}) -> p {' '.join(names)}", **dict(zip(names[1:], dims[1:])))

        x_nm = sb("x_nm", [P, TILES, FEAT], F32)
        norm = carve([CHUNKS + STEP], F32, 4)
        start_i = sb("start_i", [1, LEAD + CHUNKS], I32)
        wt = sb("wt", [FEAT, BASES, FEAT], F32)
        wcomp_bd = sb("wcomp_bd", [P, (2 * Q - 1) * Q * BASES], F32)
        loop_sb = sb("loop_sb", [FEAT, FEAT], F32)
        w1_sb = sb("w1_sb", [FEAT, FEAT], F32)
        bias0_col = sb("bias0_col", [FEAT, 1], F32)
        bias1_b = sb("bias1_b", [P, FEAT], F32)
        ident = sb("ident", [P, P], F32)
        iota_lo = sb("iota_lo", [P, P], F16)
        iota_key = sb("iota_key", [P, KEYS], F16)
        rel_id = sb("rel_id", [P, 1], F32)
        lane_i = sb("lane_i", [P, 1], I32)
        rel_id_i = sb("rel_id_i", [P, 1], I32)
        ones16 = sb("ones16", [P, 1], F16)
        eps_col = sb("eps_col", [P, 1], F32)
        neg_lo = sb("neg_lo", [P, CHUNKS + STEP], F32)
        rel = carve([CHUNKS + STEP], F32, 4)
        key = carve([CHUNKS], F32, 4)
        idx = sb("idx", [P, 2, GROUP], I32)
        rows = carve([STEP, FEAT], F32, 4)
        typ = carve([Q, P], I32, 4)
        typ_oh = carve([Q, P], F32, 4)
        coef_raw = carve([STEP * BASES], F32, 4)
        coef = carve([STEP, BASES], F32, 4)
        scat = carve([2, GROUP, BASES, WIN], F32, 4)
        key_oh = carve([2, GROUP, KEYS + WIN], F16, 2)
        win_oh = key_oh[:, :, :, KEYS:]
        lo_abs = carve([GROUP, P], F16, 2)
        lo_oh = carve([2, GROUP, P], F16, 2)
        g_sb = carve([2, BASES, GROUP * WIN], F32, 4)
        count = sb("count", [P, ROWS, NPAD], U8)
        acc = sb("acc", [FEAT, NPAD], F32)
        xt = sb("xt", [FEAT, TILES * P], F32)
        e_src, e_dst, e_to = sb("e_src", [P, 1], I32), sb("e_dst", [P, 1], I32), sb("e_to", [P, 1], I32)
        e_dstf, e_flag, e_far = sb("e_dstf", [P, 1], F32), sb("e_flag", [P, 1], F32), sb("e_far", [P, 1], F32)
        e_coef = sb("e_coef", [P, BASES], F32)
        lane, spare, least = sb("lane", [P, 1], F32), sb("spare", [P, 1], F32), sb("least", [P, 1], F32)
        tests, zero_col = sb("tests", [P, 4], F32), sb("zero_col", [P, 1], F32)
        shift_z = sb("shift_z", [P, TILES], F32)
        bad, ones32, flag = sb("bad", [P, 1], F32), sb("ones32", [P, 1], F32), sb("flag", [1, 1], I32)
        deg = sb("deg", [P, TILES], F32)
        dinv = sb("dinv", [P, TILES], F32)
        h_nm = sb("h_nm", [P, TILES, FEAT], F32)
        early = h_nm[:].rearrange("p t f -> p (t f)")[:, 0:4 * CHUNKS].bitcast(I32).rearrange("p (a k) -> p a k", a=4)
        src_i, dst_i, start_b, work_i = (early[:, n] for n in range(4))
        z_hi = sb("z_hi", [P, TILES, FEAT], F16)
        deg_part = z_hi[:].rearrange("p t f -> p (t f)")[:, 0:NPAD]
        z_lo = sb("z_lo", [P, TILES, FEAT], F16)
        stats = sb("stats", [P, TILES, 6], F32)
        mv = sb("mv", [P, TILES, 2], F32)
        rstd = sb("rstd", [P, TILES], F32)
        sdev = sb("sdev", [P, TILES], F32)
        scale_z = sb("scale_z", [P, TILES], F32)
        z_f = xt[:].rearrange("p (t f) -> p t f", f=FEAT)

        bank = [ctx.enter_context(nc.psum_tensor(f"bank{n}", [P, 512], F32)) for n in range(8)]
        cnt_ps, g_ps, z_ps = bank[0:4], bank[4:6], bank[6:8]
        coef_ps = g_ps[1][:, 4 * BASES * WIN:]

        def sems(*names):
            return [sem(n) for n in names]
        idx_loaded = sems("idx_loaded0", "idx_loaded1")
        x_loaded = sems(*(f"x_loaded{k}" for k in range(4)))
        edges_loaded, norm_loaded, types_loaded, loop_loaded, weights_loaded, zeros_loaded = sems(
            "edges_loaded", "norm_loaded", "types_loaded", "loop_loaded", "weights_loaded", "zeros_loaded")
        gathered = sems(*(f"gathered{k}" for k in range(STEP)))
        wait_carrier = sem("wait_carrier")
        iotas, wbd_zero, tail_zero, zero_col_ready, act_zeroed, chain_done, lo_nums_ready = sems(
            "iotas", "wbd_zero", "tail_zero", "zero_col_ready", "act_zeroed", "chain_done", "lo_nums_ready")
        xt_ready, xt_taken, init_ready, init_taken = sems("xt_ready", "xt_taken", "init_ready", "init_taken")
        bad_ready, bad_summed, flag_ready = sems("bad_ready", "bad_summed", "flag_ready")
        type_oh_ready, coef_ready, coef_copied, coef_taken = sems(
            "type_oh_ready", "coef_ready", "coef_copied", "coef_taken")
        win_ready, scat_ready, key_ready, lo_abs_ready, lo_ready = sems(
            "win_ready", "scat_ready", "key_ready", "lo_abs_ready", "lo_ready")
        g_ready, g_taken, z_ready, cnt_ready, counts_added, rows_added = sems(
            "g_ready", "g_taken", "z_ready", "cnt_ready", "counts_added", "rows_added")
        deg_part_ready, deg_summed, sums_ready, dinv_sqrt = sems(
            "deg_part_ready", "deg_summed", "sums_ready", "dinv_sqrt")
        turned, turned_taken, link_done, var_ready, sd_ready, scale_ready = sems(
            "turned", "turned_taken", "link_done", "var_ready", "sd_ready", "scale_ready")
        zf_ready, zhi_ready, zlo_ready, h_ready, res_ready = sems(
            "zf_ready", "zhi_ready", "zlo_ready", "h_ready", "res_ready")
        first_act, first_dve, first_pool, cnt16_act, cnt16_dve = sems(
            "first_act", "first_dve", "first_pool", "cnt16_act", "cnt16_dve")
        agg_ready, agg_done, fin_ready, fin_taken, fin_var, fin_sd, out_ready, stored = sems(
            "agg_ready", "agg_done", "fin_ready", "fin_taken", "fin_var", "fin_sd", "out_ready", "stored")
        events = ("loaded", "gathered", "turned", "xt", "types", "products", "message", "to", "summed", "total",
                  "added", "chunk_free", "cleared", "z", "dve", "back", "back_turned", "back_added", "back_taken")
        general = [{e: sem(f"general{n}_{e}") for e in events} for n in range(2)]
        clears = (TILES + 1, 2 * TILES + 1)
        sums = [nc.dram_tensor(f"sums{n}", (NODES + P, FEAT + 1 - n), F32, kind="Internal").ap() for n in range(2)]
        z_dram = nc.dram_tensor("z_dram", (NODES, FEAT), F32, kind="Internal").ap()
        e_rows, e_xt, same, earlier, before = (rows[:, n] for n in range(5))
        dst_row, e_typ, e_typ_oh = rows[:, 5].bitcast(I32), rows[0:RELS, 6].bitcast(I32), rows[0:RELS, 7]
        pair = rows[:].rearrange("p (a b) f -> p a (b f)", b=2)
        message, total = pair[:, 4], pair[:, 5]

        full = TILES - 1
        tiles = [(t, P if t < full else LAST) for t in range(TILES)]
        cuts = [0, 4, 8, 12, 16, 20, 23, TILES]
        quads = [tiles[a:b] for a, b in zip(cuts, cuts[1:])]
        blocks = [(q[0][0] * P, sum(r for _, r in q)) for q in quads]

        block = ctx.enter_context(nc.Block())

        x_parts = [(0, 8), (8, 16), (16, full)]
        count_words = count[:].rearrange("p a b -> p (a b)").bitcast(F32)

        def is_narrow(eng):
            eng.wait_ge(flag_ready, 1)
            return eng.value_load(flag[0:1, 0:1], min_val=0, max_val=1) == 0

        def general_sync(sp, layer):
            g = general[layer]
            if layer == 0:
                source = h_nm[:].rearrange("p t f -> p (t f)")[:, 0:FEAT + 1]
                sp.wait_ge(g["z"], 1)
                for t in range(TILES + 1):
                    r = min(P, NODES + P - t * P)
                    sp.dma_start(sums[0][t * P:t * P + r, :], source[0:r, :]).then_inc(g["cleared"], 16)
            else:
                sp.wait_ge(zf_ready, len(quads))
                for t, r in tiles:
                    sp.dma_start(sums[1][t * P:t * P + r, :], z_f[0:r, t, :]).then_inc(g["cleared"], 16)
                    sp.dma_start(z_dram[t * P:t * P + r, :], z_f[0:r, t, :]).then_inc(g["cleared"], 16)
                sp.dma_start(sums[1][NODES:NODES + P, :], z_f[:, 0, :]).then_inc(g["cleared"], 16)
            sp.wait_ge(g["cleared"], 16 * clears[layer])
            sp.sem_inc(g["chunk_free"], 1)
            with sp.Fori(0, CHUNKS) as k:
                sp.wait_ge(g["chunk_free"], k + 1)
                sp.dma_start(e_src[:], src_rows[bass.ds(k, 1), :].rearrange("o p -> p o")).then_inc(g["loaded"], 16)
                sp.dma_start(e_dst[:], dst_rows[bass.ds(k, 1), :].rearrange("o p -> p o")).then_inc(g["loaded"], 16)
                sp.dma_start(dst_row, dst_rows[bass.ds(k, 1), :].broadcast_to([P, P])).then_inc(g["loaded"], 16)
                sp.dma_start(e_typ, type_rows[bass.ds(k, 1), :].broadcast_to([RELS, P])).then_inc(g["loaded"], 16)
            sp.wait_ge(g["chunk_free"], CHUNKS + 1)
            width = FEAT + 1 - layer
            for t, r in tiles:
                if t:
                    sp.wait_ge(g["back_taken"], t)
                sp.dma_start(total[0:r, 0:width], sums[layer][t * P:t * P + r, :]).then_inc(g["back"], 16)

        def general_gpsimd(pool, layer):
            g = general[layer]
            table, rows_in = (x, e_rows) if layer == 0 else (z_dram, message[:, 0:FEAT])
            width = FEAT + 1 - layer
            with pool.Fori(0, CHUNKS) as k:
                pool.wait_ge(g["loaded"], 64 * k + 64)
                pool.sem_inc(wait_carrier, 1)
                pool.indirect_dma_start(rows_in, None, table[:, :],
                                        bass.IndirectOffsetOnAxis(ap=e_src[:], axis=0)).then_inc(g["gathered"], 16)
                pool.wait_ge(g["total"], k + 1)
                pool.sem_inc(wait_carrier, 1)
                pool.indirect_dma_start(sums[layer][:, :], bass.IndirectOffsetOnAxis(ap=e_to[:], axis=0),
                                        total[:, 0:width], None, compute_op=ALU.add).then_inc(g["added"], 16)
                pool.wait_ge(g["added"], 16 * k + 16)
                pool.sem_inc(g["chunk_free"], 1)

        def general_scalar(act, layer):
            g = general[layer]
            if layer == 0:
                with act.Fori(0, CHUNKS) as k:
                    act.wait_ge(g["turned"], k + 1)
                    nc.scalar.copy(e_xt, bank[0][:, 0:P]).then_inc(g["xt"], 1)

        def general_vector(v, layer):
            g = general[layer]
            width = FEAT + 1 - layer
            if layer == 0:
                nc.vector.memset(h_nm[:, 0:2, :], 0.0).then_inc(g["z"], 1)
            nc.vector.tensor_scalar(before, iota_lo[:], lane[:], None, ALU.is_lt).then_inc(g["dve"], 1)
            with v.Fori(0, CHUNKS) as k:
                n = [0]

                def link(ins):
                    n[0] += 1
                    ins.then_inc(g["dve"], 1)
                    v.wait_ge(g["dve"], steps * k + n[0] + 1)
                steps = 6 + (1 + BASES if layer == 0 else 0)
                v.wait_ge(g["loaded"], 64 * k + 64)
                link(nc.vector.tensor_copy(e_dstf[:], e_dst[:]))
                link(nc.vector.tensor_scalar(same, dst_row, e_dstf[:], None, ALU.is_equal))
                link(nc.vector.tensor_tensor(earlier, same, before, ALU.mult))
                link(nc.vector.tensor_reduce(e_flag[:], earlier, AX.X, ALU.max))
                link(nc.vector.scalar_tensor_tensor(e_flag[:], e_dstf[:], 0.0, e_flag[:], ALU.is_lt, ALU.max))
                link(nc.vector.tensor_scalar(e_far[:], e_dstf[:], -1.0, spare[:], ALU.mult, ALU.add))
                nc.vector.scalar_tensor_tensor(e_to[:], e_far[:], e_flag[:], e_dstf[:], ALU.mult,
                                               ALU.add).then_inc(g["to"], 1)
                if layer == 0:
                    nc.vector.tensor_scalar(e_typ_oh, e_typ, rel_id[0:RELS, :], None,
                                            ALU.is_equal).then_inc(g["types"], 1)
                    v.wait_ge(g["products"], k + 1)
                    link(nc.vector.tensor_scalar(e_coef[:], bank[3][:, 0:BASES], norm[:, bass.ds(k, 1)], None,
                                                 ALU.mult))
                    for b in range(BASES):
                        product = bank[1 + b // 4][:, (b % 4) * FEAT:(b % 4 + 1) * FEAT]
                        if b == 0:
                            link(nc.vector.tensor_scalar(message[:, 0:FEAT], product, e_coef[:, 0:1], None, ALU.mult))
                        else:
                            link(nc.vector.scalar_tensor_tensor(message[:, 0:FEAT], product, e_coef[:, b:b + 1],
                                                                message[:, 0:FEAT], ALU.mult, ALU.add))
                    nc.vector.tensor_scalar(message[:, FEAT:FEAT + 1], e_dstf[:], 0.0, None,
                                            ALU.is_ge).then_inc(g["message"], 1)
                assert n[0] == steps
                v.wait_ge(g["summed"], k + 1)
                v.wait_ge(g["to"], k + 1)
                nc.vector.tensor_copy(total[:, 0:width], bank[4][:, 0:width]).then_inc(g["total"], 1)
            for t, r in tiles:
                v.wait_ge(g["back_turned"], t + 1)
                to, ps = acc[:, t * P:t * P + r], bank[t % 2][:, 0:r]
                if layer == 0:
                    nc.vector.tensor_scalar(to, ps, bias0_col[:], None, ALU.add).then_inc(g["back_added"], 1)
                    v.wait_ge(g["back"], 16 * t + 16)
                    nc.vector.tensor_scalar(deg[0:r, t:t + 1], total[0:r, FEAT:FEAT + 1], 1.0, None,
                                            ALU.add).then_inc(g["back_taken"], 1)
                else:
                    nc.vector.tensor_scalar(to, ps, 1.0 / ZSCALE, None, ALU.mult).then_inc(g["back_added"], 1)
                    nc.vector.engine_nop().then_inc(g["back_taken"], 1)
            v.wait_ge(g["back_added"], TILES)

        def general_tensor(pe, layer):
            g = general[layer]
            width = FEAT + 1 - layer
            with pe.Fori(0, CHUNKS) as k:
                pe.wait_ge(g["gathered"], 16 * k + 16)
                if layer == 0:
                    nc.tensor.transpose(bank[0][:, 0:P], e_rows, ident[:]).then_inc(g["turned"], 1)
                    pe.wait_ge(g["types"], k + 1)
                    at = (Q - 1) * Q * BASES
                    nc.tensor.matmul(bank[3][:, 0:BASES], e_typ_oh, wcomp_bd[0:RELS, at:at + BASES],
                                     start=True, stop=True)
                    pe.wait_ge(g["xt"], k + 1)
                    for half in range(2):
                        last = nc.tensor.matmul(bank[1 + half][:], e_xt,
                                                wt[:, 4 * half:4 * half + 4, :].rearrange("p b f -> p (b f)"),
                                                start=True, stop=True)
                    last.then_inc(g["products"], 1)
                    pe.wait_ge(g["message"], k + 1)
                else:
                    pe.wait_ge(g["to"], k + 1)
                nc.tensor.matmul(bank[4][:, 0:width], same, message[:, 0:width],
                                 start=True, stop=True).then_inc(g["summed"], 1)
            for t, r in tiles:
                pe.wait_ge(g["back"], 16 * t + 16)
                if t >= 2:
                    pe.wait_ge(g["back_added"], t - 1)
                last = nc.tensor.matmul(bank[t % 2][:, 0:r], total[0:r, 0:FEAT], ident[0:r, 0:r], start=True,
                                        stop=(layer == 1))
                if layer == 0:
                    last = nc.tensor.matmul(bank[t % 2][:, 0:r], loop_sb[:], xt[:, t * P:t * P + r],
                                            start=False, stop=True)
                last.then_inc(g["back_turned"], 1)

        @block.sync
        def _(sp):
            def load_idx(i, h):
                sp.dma_start(idx[:, h, :],
                             src_idx[bass.ds(i, 1), h].rearrange("o p k -> (o p) k")).then_inc(idx_loaded[h], 16)

            def load_types(i):
                for q in range(Q):
                    sp.dma_start(typ[RELS * q:RELS * (q + 1), :, :].rearrange("p a b -> p (a b)"),
                                 types[bass.ds(i, 1), q].rearrange("o u n -> (o u) n").broadcast_to([RELS, Q * P])
                                 ).then_inc(types_loaded, 16)

            sp.dma_start(idx[:, 0, :], src_idx[0, 0]).then_inc(idx_loaded[0], 16)
            sp.dma_start(src_i, src_t).then_inc(edges_loaded, 16)
            sp.dma_start(dst_i, dst_t).then_inc(edges_loaded, 16)
            sp.dma_start(start_b, starts[:, LEAD:LEAD + CHUNKS].broadcast_to([P, CHUNKS])).then_inc(edges_loaded, 16)
            sp.wait_ge(tail_zero, 1)
            for part, (a, b) in enumerate(x_parts):
                if part == 1:
                    sp.dma_start(loop_sb[:], loop_w).then_inc(loop_loaded, 16)
                    sp.dma_start(bias0_col[:], bias0.rearrange("(f o) -> f o", o=1)).then_inc(loop_loaded, 16)
                sp.dma_start(x_nm[:, a:b, :],
                             x[a * P:b * P, :].rearrange("(t p) f -> p t f", p=P)).then_inc(x_loaded[part], 16)
            sp.dma_start(x_nm[0:LAST, full, :], x[full * P:NODES, :]).then_inc(x_loaded[-1], 16)
            sp.dma_start(idx[:, 1, :], src_idx[0, 1]).then_inc(idx_loaded[1], 16)
            load_types(0)
            sp.wait_ge(g_taken, 4)
            for k in range(ZERO_DMAS):
                at = ZERO_ACT + ZERO_DVE + k * ZERO_DMA
                sp.dma_start(count_words[:, at:at + ZERO_DMA],
                             g_sb[:].rearrange("p h b n -> p (h b n)")).then_inc(zeros_loaded, 16)
            sp.dma_start(start_i[:], starts).then_inc(norm_loaded, 16)
            sp.dma_start(norm[:, 0:CHUNKS], norm_t).then_inc(norm_loaded, 16)
            sp.wait_ge(wbd_zero, 1)
            for q in range(Q):
                at = (Q - 1) * Q * BASES + BASES * q
                sp.dma_start(wcomp_bd[RELS * q:RELS * (q + 1), at:at + BASES], w_comp).then_inc(weights_loaded, 16)
            sp.dma_start(wt[:], weight.rearrange("b d f -> d b f")).then_inc(weights_loaded, 16)
            sp.dma_start(w1_sb[:], w1).then_inc(weights_loaded, 16)
            sp.dma_start(bias1_b[:],
                         bias1.rearrange("(o f) -> o f", o=1).broadcast_to([P, FEAT])).then_inc(weights_loaded, 16)
            with sp.Fori(0, STEPS) as i:
                sp.wait_ge(type_oh_ready, i + 1)
                load_types(i + 1)
                for h in range(2):
                    for j in range(GROUP * h, GROUP * h + GROUP):
                        sp.wait_ge(gathered[j], 16 * i + 16)
                    load_idx(i + 1, h)
            with sp.If(is_narrow(sp)):
                sp.wait_ge(flag_ready, 1)
            with sp.Else():
                general_sync(sp, 0)
                general_sync(sp, 1)
            for n, quad in enumerate(quads):
                sp.wait_ge(out_ready, n + 1)
                whole = [t for t, r in quad if r == P]
                a, b = whole[0], whole[-1] + 1
                sp.dma_start(out[a * P:b * P, :].rearrange("(t p) f -> p t f", p=P),
                             x_nm[:, a:b, :]).then_inc(stored, 16)
            sp.dma_start(out[full * P:NODES, :], x_nm[0:LAST, full, :]).then_inc(stored, 16)
            sp.wait_ge(stored, 16 * (len(quads) + 1))

        @block.gpsimd
        def _(pool):
            def gather(j):
                return pool.indirect_dma_start(
                    rows[:, j, :], None, x[:, :],
                    bass.IndirectOffsetOnAxis(ap=idx[:, j // GROUP, j % GROUP:j % GROUP + 1], axis=0)
                    ).then_inc(gathered[j], 16)

            nc.gpsimd.memset(g_sb[:], 0.0).then_inc(g_taken, 4)
            nc.gpsimd.iota(lane_i[:], [[0, 1]], base=0, channel_multiplier=1)
            nc.gpsimd.iota(iota_lo[:], [[1, P]], base=0, channel_multiplier=0, allow_small_or_imprecise_dtypes=True)
            nc.gpsimd.iota(iota_key[:], [[1, KEYS]], base=0, channel_multiplier=0,
                           allow_small_or_imprecise_dtypes=True).then_inc(iotas, 1)
            nc.gpsimd.memset(ident[:], 1.0).then_inc(iotas, 1)
            pool.wait_ge(iotas, 2)
            nc.gpsimd.affine_select(out=ident[:], in_=ident[:], compare_op=ALU.is_equal, fill=0.0, base=0,
                                    pattern=[[-1, P]], channel_multiplier=1).then_inc(iotas, 1)
            for h in range(2):
                pool.wait_ge(idx_loaded[h], 16)
                for j in range(GROUP * h, GROUP * h + GROUP):
                    gather(j)
            with pool.Fori(1, STEPS) as i:
                for h in range(2):
                    pool.wait_ge(idx_loaded[h], 16 * i + 16)
                    for j in range(GROUP * h, GROUP * h + GROUP):
                        pool.wait_ge(cnt_ready, STEP * i - STEP + j + 1 + LAG)
                        pool.sem_inc(wait_carrier, 1)
                        gather(j)

            def add_bias():
                pool.wait_ge(weights_loaded, 16 * (Q + 3))
                for n, quad in enumerate(quads):
                    t0, k = quad[0][0], len(quad)
                    pool.wait_ge(h_ready, n + 1)
                    nc.gpsimd.tensor_tensor(h_nm[:, t0:t0 + k], h_nm[:, t0:t0 + k],
                                            bias1_b[:].unsqueeze(1).broadcast_to([P, k, FEAT]),
                                            ALU.add).then_inc(res_ready, 1)

            with pool.If(is_narrow(pool)):
                pool.wait_ge(z_ready, 2 * STEPS + 2)
                pool.wait_ge(counts_added, CHUNKS + LAG + 2)
                for row in range(FIRST_ROWS, TILES - FIRST_DVE):
                    ins = nc.gpsimd.tensor_copy(cnt16[:, 0, row, :], count[:, row, 0:BLOCK])
                ins.then_inc(first_pool, 1)
                for n, quad in enumerate(quads):
                    t0, k = quad[0][0], len(quad)
                    pool.wait_ge(zhi_ready, n + 1)
                    nc.gpsimd.tensor_tensor(z_lo[:, t0:t0 + k], z_f[:, t0:t0 + k], z_hi[:, t0:t0 + k],
                                            ALU.subtract).then_inc(zlo_ready, 1)
                add_bias()
            with pool.Else():
                general_gpsimd(pool, 0)
                add_bias()
                general_gpsimd(pool, 1)

        @block.scalar
        def _(act):
            def deviation(to, n, ready, done):
                t0, k = quads[n][0][0], len(quads[n])
                act.wait_ge(ready, n + 1)
                nc.scalar.activation(to[:, t0:t0 + k], mv[:, t0:t0 + k, 1], ACT.Sqrt,
                                     bias=eps_col[:]).then_inc(done, 1)

            def one_hot_lo(g, h, n):
                if not isinstance(n, int):
                    act.wait_ge(lo_ready, n - 1)
                for j in range(GROUP):
                    last = nc.scalar.activation(lo_abs[:, j, :], iota_lo[:], ACT.Abs,
                                                bias=neg_lo[:, bass.ds(GROUP * g + j, 1)])
                last.then_inc(lo_abs_ready, 1)
                act.wait_ge(lo_abs_ready, n)
                nc.scalar.activation(lo_oh[:, h], lo_abs[:], ACT.Relu, bias=1.0, scale=-1.0).then_inc(lo_ready, 1)

            act.wait_ge(zero_col_ready, 1)
            nc.scalar.activation(count_words[:, 0:ZERO_ACT], zero_col[:].broadcast_to([P, ZERO_ACT]),
                                 ACT.Copy).then_inc(act_zeroed, 1)

            def loop_bias(n):
                a, width = blocks[n]
                act.wait_ge(init_ready, n + 1)
                nc.scalar.activation(acc[:, a:a + width], bank[2 + n % 2][:, 0:width], ACT.Identity,
                                     bias=bias0_col[:]).then_inc(init_taken, 1)

            for n, (a, width) in enumerate(blocks):
                act.wait_ge(xt_ready, n + 1)
                nc.scalar.copy(xt[:, a:a + width], bank[n % 2][:, 0:width]).then_inc(xt_taken, 1)
                if n == 0:
                    act.wait_ge(iotas, 1)
                    act.wait_ge(lo_nums_ready, 1)
                    one_hot_lo(0, 0, 1)
                    act.wait_ge(loop_loaded, 32)
                else:
                    loop_bias(n - 1)
                if n == len(blocks) - 2:
                    act.wait_ge(coef_ready, 1)
                    nc.scalar.copy(coef_raw[:], coef_ps[:]).then_inc(coef_copied, 1)
            loop_bias(len(blocks) - 1)
            act.wait_ge(coef_copied, 1)
            with act.Fori(0, STEPS) as i:
                for h in range(2):
                    g = 2 * i + h
                    act.wait_ge(cnt_ready, GROUP * g + LAG)
                    one_hot_lo(g + 1, 1 - h, g + 2)
                    act.wait_ge(z_ready, g + 1)
                    for q in range(2):
                        act.wait_ge(g_ready, 2 * g + q + 1)
                        if h == 0 and q == 1:
                            act.wait_ge(coef_taken, i + 1)
                            nc.scalar.copy(coef_raw[:], coef_ps[:]).then_inc(coef_copied, 1)
                        nc.scalar.copy(g_sb[:, h].rearrange("p b (c n) -> p c b n", n=WIN)[:, 4 * q:4 * q + 4],
                                       g_ps[q][:, 0:4 * BASES * WIN].rearrange("p (c b n) -> p c b n", b=BASES, n=WIN)
                                       ).then_inc(g_taken, 1)

            def convert(n):
                a, width = blocks[n]
                if n >= 2:
                    act.wait_ge(agg_ready, n - 1)
                nc.scalar.copy(cnt16[:, n % 2, 0:ACT_ROWS[n], 0:width],
                               count[:, 0:ACT_ROWS[n], a:a + width]).then_inc(cnt16_act, 1)

            def first_end(fast):
                act.wait_ge(sums_ready, 1 if fast else 2)
                nc.scalar.activation(dinv[:], deg[:], ACT.Sqrt).then_inc(dinv_sqrt, 1)

                def z_part(n):
                    quad = quads[n]
                    t0, k = quad[0][0], len(quad)
                    act.wait_ge(scale_ready, n + 1)
                    for t, _ in quad:
                        last = nc.scalar.activation(z_f[:, t, :], x_nm[:, t, :], ACT.Identity,
                                                    bias=shift_z[:, t:t + 1], scale=scale_z[:, t:t + 1])
                    last.then_inc(zf_ready, 1)
                    if fast:
                        act.wait_ge(zf_ready, n + 1)
                        nc.scalar.copy(z_hi[:, t0:t0 + k], z_f[:, t0:t0 + k]).then_inc(zhi_ready, 1)

                for n in range(len(quads)):
                    deviation(sdev, n, var_ready, sd_ready)
                    if n:
                        z_part(n - 1)
                z_part(len(quads) - 1)

            with act.If(is_narrow(act)):
                act.wait_ge(z_ready, 2 * STEPS + 2)
                act.wait_ge(counts_added, CHUNKS + LAG + 2)
                nc.scalar.copy(cnt16[:, 0, 0:FIRST_ROWS, :], count[:, 0:FIRST_ROWS, 0:BLOCK]).then_inc(first_act, 1)
                first_end(True)
                convert(1)
                for n, (a, width) in enumerate(blocks):
                    act.wait_ge(agg_ready, n + 1)
                    nc.scalar.activation(acc[:, a:a + width], bank[4 + n % 2][:, 0:width], ACT.Copy,
                                         scale=1.0 / ZSCALE).then_inc(agg_done, 1)
                    if n + 2 < len(blocks):
                        convert(n + 2)
                    deviation(sdev, n, fin_var, fin_sd)
            with act.Else():
                general_scalar(act, 0)
                first_end(False)
                for n in range(len(blocks)):
                    deviation(sdev, n, fin_var, fin_sd)

        @block.vector
        def _(v):
            chained = [0]

            def chain(ins):
                chained[0] += 1
                ins.then_inc(chain_done, 1)
                v.wait_ge(chain_done, chained[0])

            nc.vector.memset(x_nm[:, full, :], 0.0).then_inc(tail_zero, 1)
            nc.vector.memset(zero_col[:], 0.0).then_inc(zero_col_ready, 1)
            nc.vector.memset(wcomp_bd[:], 0.0).then_inc(wbd_zero, 1)
            nc.vector.memset(eps_col[:], EPS)
            nc.vector.memset(ones16[:], 1.0)
            nc.vector.memset(ones32[:], 1.0)
            for padded in (neg_lo, rel, norm):
                nc.vector.memset(padded[:, CHUNKS:], 0.0)
            nc.vector.memset(deg[:], 1.0)
            nc.vector.memset(mv[:], 1.0)
            nc.vector.memset(acc[:, NODES:], 0.0).then_inc(rows_added, 1)
            split, rest = ZERO_ACT + ZERO_DVE, ZERO_ACT + ZERO_DVE + ZERO_DMAS * ZERO_DMA
            nc.vector.memset(count_words[:, ZERO_ACT:split], 0.0)
            v.wait_ge(iotas, 1)
            chain(nc.vector.tensor_scalar(rel_id_i[:], lane_i[:], RELS - 1, None, ALU.bitwise_and))
            nc.vector.tensor_copy(lane[:], lane_i[:])
            nc.vector.tensor_copy(rel_id[:], rel_id_i[:])
            v.wait_ge(edges_loaded, 48)
            chain(nc.vector.tensor_scalar(work_i, src_i, P - 1, None, ALU.bitwise_and))
            nc.vector.tensor_scalar(neg_lo[:, 0:CHUNKS], work_i, -1.0, None, ALU.mult).then_inc(lo_nums_ready, 1)
            v.wait_ge(lo_nums_ready, 1)
            chain(nc.vector.tensor_tensor(rel[:, 0:CHUNKS], dst_i, start_b, ALU.subtract))
            chain(nc.vector.tensor_scalar(work_i, src_i, 7, None, ALU.logical_shift_right))
            chain(nc.vector.scalar_tensor_tensor(key[:], work_i, float(WIN), rel[:, 0:CHUNKS], ALU.mult, ALU.add))

            def type_one_hot(i):
                v.wait_ge(types_loaded, 64 * i + 64)
                nc.vector.tensor_scalar(typ_oh[:], typ[:], rel_id[:], None, ALU.is_equal).then_inc(type_oh_ready, 1)

            nc.vector.memset(count_words[:, rest:], 0.0).then_inc(counts_added, 1)
            type_one_hot(0)
            v.wait_ge(counts_added, 1)
            v.wait_ge(act_zeroed, 1)
            v.wait_ge(zeros_loaded, 16 * ZERO_DMAS)
            v.wait_ge(iotas, 3)
            squares = count[:].rearrange("p r n -> p (r n)")[:, 0:full * (NPAD + P)]
            squares = squares.rearrange("p (t w) -> p t w", t=full)
            nc.vector.tensor_copy(squares[:, :, 0:P], ident[:].unsqueeze(1).broadcast_to([P, full, P]))
            nc.vector.tensor_copy(count[:, full, full * P:NODES], ident[:, 0:LAST]).then_inc(counts_added, 1)
            v.wait_ge(counts_added, 2)
            n = CHUNKS - 1
            over = h_nm[:].rearrange("p t f -> p (t f)")[:, 4 * CHUNKS:5 * CHUNKS]
            nc.vector.tensor_scalar(least[:], lane[:], P - 1, None, ALU.is_equal)
            nc.vector.tensor_scalar(spare[:], lane[:], float(NODES), None, ALU.add)
            nc.vector.tensor_reduce(tests[:, 0:1], rel[:, 0:CHUNKS], AX.X, ALU.max)
            nc.vector.tensor_reduce(tests[:, 1:2], rel[:, 0:n], AX.X, ALU.min)
            nc.vector.tensor_tensor(over[:, 0:n], dst_i[:, 0:n], start_b[:, 1:CHUNKS], ALU.subtract)
            chain(nc.vector.tensor_scalar(tests[:, 3:4], dst_i[:, n:CHUNKS], 0.0, None, ALU.is_ge))
            nc.vector.scalar_tensor_tensor(tests[:, 3:4], rel[:, n:CHUNKS], 0.0, tests[:, 3:4], ALU.is_lt, ALU.mult)
            nc.vector.tensor_reduce(tests[:, 2:3], over[:, 0:n], AX.X, ALU.max)
            nc.vector.tensor_scalar(tests[:, 0:1], tests[:, 0:1], float(WIN), None, ALU.is_ge)
            chain(nc.vector.tensor_scalar(tests[:, 1:2], tests[:, 1:2], least[:], None, ALU.is_lt))
            chain(nc.vector.tensor_scalar(tests[:, 2:3], tests[:, 2:3], 0.0, None, ALU.is_gt))
            nc.vector.tensor_reduce(bad[:], tests[:], AX.X, ALU.max).then_inc(bad_ready, 1)
            v.wait_ge(norm_loaded, 32)

            def add_counts(start, c, j, n):
                v.wait_ge(cnt_ready, c)
                v.wait_ge(counts_added, n)
                w = count[:, :, bass.ds(start, WIN)]
                nc.vector.tensor_tensor(w, w, cnt_ps[j % 4][:, 0:ROWS * WIN].rearrange("p (r n) -> p r n", n=WIN),
                                        ALU.add).then_inc(counts_added, 1)

            def add_rows(start, h, k, n):
                v.wait_ge(rows_added, n)
                w = acc[:, bass.ds(start, WIN)]
                nc.vector.tensor_tensor(w, w, z_ps[h][:, k * WIN:(k + 1) * WIN], ALU.add).then_inc(rows_added, 1)

            def load_starts(at, n):
                _, vals = nc.values_load_multi_w_load_instructions(
                    start_i[0:1, bass.ds(at, n)], engines=[mybir.EngineType.DVE], min_val=0, max_val=NODES - 1,
                    skip_runtime_bounds_check_because="window starts are destination nodes, below 3125")
                return vals

            def coefficients(i):
                v.wait_ge(coef_copied, i + 1)
                nc.vector.tensor_tensor(
                    coef[:].rearrange("p (q j) b -> p q j b", q=Q),
                    coef_raw[:].rearrange("p (j q b) -> p q j b", q=Q, b=BASES),
                    norm[:, bass.ds(STEP * i, STEP)].rearrange("p (q j) -> p q j", q=Q).unsqueeze(3)
                    .broadcast_to([P, Q, Q, BASES]),
                    ALU.mult).then_inc(coef_taken, 1)

            def window_one_hot(g, h):
                nc.vector.tensor_tensor(
                    win_oh[:, h], iota_key[:, 0:WIN].unsqueeze(1).broadcast_to([P, GROUP, WIN]),
                    rel[:, bass.ds(GROUP * g, GROUP)].unsqueeze(2).broadcast_to([P, GROUP, WIN]),
                    ALU.is_equal).then_inc(win_ready, 1)

            def scatter(g, h, steps_taken):
                v.wait_ge(win_ready, g + 1)
                v.wait_ge(coef_taken, steps_taken)
                nc.vector.tensor_tensor(
                    scat[:, h], win_oh[:, h].unsqueeze(2).broadcast_to([P, GROUP, BASES, WIN]),
                    coef[:, GROUP * h:GROUP * (h + 1), :].unsqueeze(3).broadcast_to([P, GROUP, BASES, WIN]),
                    ALU.mult).then_inc(scat_ready, 1)

            window_one_hot(0, 0)
            v.wait_ge(bad_summed, 1)
            nc.vector.tensor_scalar(flag[:], bank[4][0:1, 0:1], 1.0, None, ALU.min).then_inc(flag_ready, 1)
            coefficients(0)
            scatter(0, 0, 1)
            v.wait_ge(init_taken, len(blocks))
            with v.Fori(0, STEPS) as i:
                for h in range(2):
                    g = 2 * i + h
                    a_start = load_starts(GROUP * g, GROUP)
                    c_start = load_starts(GROUP * g + LEAD - LAG, GROUP)
                    for j in range(GROUP):
                        c = GROUP * g + j
                        nc.vector.tensor_scalar(key_oh[:, h, j, 0:KEYS], iota_key[:], key[:, bass.ds(c, 1)], None,
                                                ALU.is_equal).then_inc(key_ready, 1)
                        if j == 0:
                            v.wait_ge(z_ready, g + 1)
                        add_rows(a_start[j], h, j, c + 1)
                        add_counts(c_start[j], c + 1, j - LAG, c + 2)
                        if j == 0 and h == 0:
                            type_one_hot(i + 1)
                        if j == 3 and h == 1:
                            coefficients(i + 1)
                        if j == 3:
                            window_one_hot(g + 1, 1 - h)
                        if j == 4:
                            scatter(g + 1, 1 - h, i + 1 + h)

            def last_sums():
                c_start = load_starts(CHUNKS + LEAD - LAG, LAG)
                for k in range(LAG):
                    add_counts(c_start[k], CHUNKS + k + 1, k - LAG, CHUNKS + k + 2)
                n = CHUNKS + 1
                part = NPAD // GROUP
                for g in (2 * STEPS, 2 * STEPS + 1):
                    a_start = load_starts(GROUP * g, GROUP)
                    v.wait_ge(z_ready, g + 1)
                    for k in range(GROUP):
                        add_rows(a_start[k], g % 2, k, n)
                        n += 1
                        if g == 2 * STEPS:
                            if k == 0:
                                v.wait_ge(counts_added, CHUNKS + LAG + 2)
                            ins = nc.vector.tensor_copy(deg_part[:, part * k:part * (k + 1)],
                                                        count[:, TILES, part * k:part * (k + 1)])
                            if k == GROUP - 1:
                                ins.then_inc(deg_part_ready, 1)
                        else:
                            row, half = TILES - FIRST_DVE + k // 2, BLOCK // 2 * (k % 2)
                            ins = nc.vector.tensor_copy(cnt16[:, 0, row, half:half + BLOCK // 2],
                                                        count[:, row, half:half + BLOCK // 2])
                            if k == GROUP - 1:
                                ins.then_inc(first_dve, 1)
                assert part * GROUP == NPAD and 2 * FIRST_DVE == GROUP
                v.wait_ge(deg_summed, 1)
                nc.vector.tensor_scalar(deg[:, 0:full], bank[1][:, 0:full], 1.0, None, ALU.add)
                nc.vector.tensor_scalar(deg[0:LAST, full:TILES], bank[1][0:LAST, full:TILES], 1.0, None,
                                        ALU.add).then_inc(sums_ready, 1)

            links = [0]

            def link(ins):
                links[0] += 1
                ins.then_inc(link_done, 1)
                v.wait_ge(link_done, links[0])

            def flat(ap):
                return ap.rearrange("p a b -> p (a b)")

            def first_end():
                def numbers(n):
                    t0, k = quads[n][0][0], len(quads[n])
                    to = slice(t0, t0 + k)
                    v.wait_ge(sd_ready, n + 1)
                    link(nc.vector.reciprocal(rstd[:, to], sdev[:, to]))
                    link(nc.vector.scalar_tensor_tensor(scale_z[:, to], rstd[:, to], ZSCALE, dinv[:, to],
                                                        ALU.mult, ALU.mult))
                    nc.vector.scalar_tensor_tensor(shift_z[:, to], mv[:, to, 0], -1.0, scale_z[:, to],
                                                   ALU.mult, ALU.mult).then_inc(scale_ready, 1)

                for n, quad in enumerate(quads):
                    v.wait_ge(turned, n + 1)
                    t0, k, r = quad[0][0], len(quad), quad[0][1]
                    whole = [q for q in quad if q[1] == P]
                    for a, m, r in ((t0, len(whole), P), (full, k - len(whole), LAST)):
                        if m:
                            ins = nc.vector.scalar_tensor_tensor(
                                flat(x_nm[0:r, a:a + m, :]), bank[n % 4][0:r, (a - t0) * FEAT:(a - t0 + m) * FEAT], 0.0,
                                flat(x_nm[0:r, a:a + m, :]), ALU.max, ALU.add)
                    ins.then_inc(turned_taken, 1)
                    v.wait_ge(turned_taken, n + 1)
                    for t, r in quad:
                        ins = nc.vector.bn_stats(stats[0:r, t, :], x_nm[0:r, t, :])
                    link(ins)
                    for t, r in quad:
                        ins = nc.vector.bn_aggr(mv[0:r, t, :], stats[0:r, t, :])
                    ins.then_inc(var_ready, 1)
                    if n == 0:
                        v.wait_ge(dinv_sqrt, 1)
                        link(nc.vector.reciprocal(dinv[:], dinv[:]))
                    else:
                        numbers(n - 1)
                numbers(len(quads) - 1)

            def residual():
                for n, quad in enumerate(quads):
                    for t, r in quad:
                        ins = nc.vector.tensor_scalar(h_nm[:, t, :], x_nm[:, t, :], mv[:, t, 0:1], rstd[:, t:t + 1],
                                                      ALU.subtract, ALU.mult)
                    ins.then_inc(h_ready, 1)

            def convert(n):
                a, width = blocks[n]
                if n >= 2:
                    v.wait_ge(agg_ready, n - 1)
                nc.vector.tensor_copy(cnt16[:, n % 2, ACT_ROWS[n]:TILES, 0:width],
                                      count[:, ACT_ROWS[n]:TILES, a:a + width]).then_inc(cnt16_dve, 1)

            def finish(n):
                quad = quads[n]
                t0, k = quad[0][0], len(quad)
                v.wait_ge(res_ready, n + 1)
                v.wait_ge(fin_ready, n + 1)
                for t, r in quad:
                    ins = nc.vector.scalar_tensor_tensor(
                        h_nm[0:r, t, :], bank[6 + n % 2][0:r, (t - t0) * FEAT:(t - t0 + 1) * FEAT], dinv[0:r, t:t + 1],
                        h_nm[0:r, t, :], ALU.mult, ALU.add)
                ins.then_inc(fin_taken, 1)
                v.wait_ge(fin_taken, n + 1)
                for t, r in quad:
                    ins = nc.vector.bn_stats(stats[0:r, t, :], h_nm[0:r, t, :])
                link(ins)
                for t, r in quad:
                    ins = nc.vector.bn_aggr(mv[0:r, t, :], stats[0:r, t, :])
                ins.then_inc(fin_var, 1)
                v.wait_ge(fin_sd, n + 1)
                link(nc.vector.reciprocal(rstd[:, t0:t0 + k], sdev[:, t0:t0 + k]))
                for t, r in quad:
                    ins = nc.vector.tensor_scalar(x_nm[0:r, t, :], h_nm[0:r, t, :], mv[0:r, t, 0:1], rstd[0:r, t:t + 1],
                                                  ALU.subtract, ALU.mult)
                ins.then_inc(out_ready, 1)

            last_sums()
            narrow = is_narrow(v)
            with v.If(narrow):
                first_end()
                convert(1)
                residual()
                for n in range(len(blocks)):
                    if n + 2 < len(blocks):
                        convert(n + 2)
                    finish(n)
            with v.Else():
                links[0] = 0
                general_vector(v, 0)
                nc.vector.engine_nop().then_inc(sums_ready, 1)
                first_end()
                residual()
                general_vector(v, 1)
                nc.vector.engine_nop().then_inc(agg_done, len(blocks))
                for n in range(len(blocks)):
                    finish(n)

        @block.tensor
        def _(pe):
            pe.wait_ge(iotas, 3)

            def turn_x(n):
                if n % 2 == 0:
                    pe.wait_ge(x_loaded[n // 2], 16)
                if n >= 2:
                    pe.wait_ge(xt_taken, n - 1)
                for t, r in quads[n]:
                    c = (t - quads[n][0][0]) * P
                    last = nc.tensor.transpose(bank[n % 2][:, c:c + r], x_nm[0:r, t, :], ident[0:r, 0:r])
                last.then_inc(xt_ready, 1)

            def loop_product(n):
                a, width = blocks[n]
                pe.wait_ge(xt_taken, n + 1)
                if n >= 2:
                    pe.wait_ge(init_taken, n - 1)
                nc.tensor.matmul(bank[2 + n % 2][:, 0:width], loop_sb[:], xt[:, a:a + width],
                                 start=True, stop=True).then_inc(init_ready, 1)

            def second_product(h, b):
                last = nc.tensor.matmul(z_ps[h][:, 0:GROUP * WIN], wt[:, b, :], g_sb[:, h, b, :],
                                        start=(b == 0), stop=(b == BASES - 1))
                if b == BASES - 1:
                    last.then_inc(z_ready, 1)

            def look_up(i):
                pe.wait_ge(type_oh_ready, i + 1)
                for j in range(Q):
                    at = (Q - 1 - j) * Q * BASES
                    last = nc.tensor.matmul(coef_ps[:], typ_oh[:, j, :], wcomp_bd[:, at:at + Q * Q * BASES],
                                            start=(j == 0), stop=(j == Q - 1))
                return last

            turn_x(0)
            for n in range(1, len(quads)):
                turn_x(n)
                if n == 1:
                    pe.wait_ge(loop_loaded, 32)
                loop_product(n - 1)
                if n == len(quads) - 2:
                    pe.wait_ge(weights_loaded, 16 * (Q + 3))
                    look_up(0).then_inc(coef_ready, 1)
            loop_product(len(quads) - 1)
            pe.wait_ge(bad_ready, 1)
            nc.tensor.matmul(bank[4][0:1, 0:1], bad[:], ones32[:], start=True, stop=True).then_inc(bad_summed, 1)
            pe.wait_ge(coef_copied, 1)
            pe.wait_ge(g_taken, 4)
            for b in range(BASES):
                second_product(0, b)
            pe.wait_ge(init_taken, len(blocks))
            zeros = g_sb[:, 0].rearrange("p b n -> p (b n)")
            for k in range(LAG):
                nc.tensor.matmul(cnt_ps[4 - LAG + k][:, 0:ROWS * WIN], zeros[:, 0:P], zeros[:, 0:ROWS * WIN],
                                 start=True, stop=True).then_inc(cnt_ready, 1)
            pe.wait_ge(flag_ready, 1)
            with pe.Fori(0, STEPS) as i:
                for h in range(2):
                    g = 2 * i + h
                    for j in range(GROUP):
                        q, jj, c = j // 4, j % 4, GROUP * g + j
                        if j == 0:
                            pe.wait_ge(scat_ready, g + 1)
                        if jj == 0:
                            pe.wait_ge(g_taken, 2 * g + q + 3)
                        if j == 4 and h == 0:
                            look_up(i + 1)
                        pe.wait_ge(gathered[GROUP * h + j], 16 * i + 16)
                        last = nc.tensor.matmul(g_ps[q][:, jj * BASES * WIN:(jj + 1) * BASES * WIN],
                                                rows[:, GROUP * h + j, :],
                                                scat[:, h, j].rearrange("p b n -> p (b n)"), start=True, stop=True)
                        if jj == 3:
                            last.then_inc(g_ready, 1)
                        if j == 1:
                            pe.wait_ge(g_taken, 2 * g + 4)
                            pe.wait_ge(rows_added, GROUP * g + 1)
                        for b in range(BASES)[max(j - 1, 0):j + j // (GROUP - 1)]:
                            second_product(1 - h, b)
                        pe.wait_ge(key_ready, c + 1)
                        if j == 0:
                            pe.wait_ge(lo_ready, g + 1)
                        pe.wait_ge(counts_added, c + 1)
                        nc.tensor.matmul(cnt_ps[j % 4][:, 0:KEYS + WIN], lo_oh[:, h, j, :], key_oh[:, h, j, :],
                                         start=True, stop=True).then_inc(cnt_ready, 1)

            def first_end(fast):
                for n, quad in enumerate(quads):
                    if n >= 4:
                        pe.wait_ge(turned_taken, n - 3)
                    for t, r in quad:
                        c = (t - quad[0][0]) * P
                        last = nc.tensor.transpose(bank[n % 4][0:r, c:c + P], acc[:, t * P:t * P + r], ident[:])
                    last.then_inc(turned, 1)
                if fast:
                    for n in range(len(quads)):
                        first_block(n)

            def pair_products(n, t):
                width = blocks[n][1]
                for half in (z_hi, z_lo):
                    last = nc.tensor.matmul(bank[4 + n % 2][:, 0:width], half[:, t, :], cnt16[:, n % 2, t, 0:width],
                                            start=(t == 0 and half is z_hi), stop=(t == TILES - 1 and half is z_lo))
                return last

            def first_block(q):
                pe.wait_ge(zlo_ready, q + 1)
                for t, _ in quads[q]:
                    if t == 0:
                        pe.wait_ge(first_act, 1)
                    elif t == FIRST_ROWS:
                        pe.wait_ge(first_pool, 1)
                    elif t == TILES - FIRST_DVE:
                        pe.wait_ge(first_dve, 1)
                    last = pair_products(0, t)
                if q == len(quads) - 1:
                    last.then_inc(agg_ready, 1)

            def project(n):
                pe.wait_ge(agg_done, n + 1)
                if n >= 2:
                    pe.wait_ge(fin_taken, n - 1)
                for t, r in quads[n]:
                    c = (t - quads[n][0][0]) * FEAT
                    last = nc.tensor.matmul(bank[6 + n % 2][0:r, c:c + FEAT], acc[:, t * P:t * P + r], w1_sb[:],
                                            start=True, stop=True)
                last.then_inc(fin_ready, 1)

            pe.wait_ge(g_taken, 4 * STEPS + 4)
            pe.wait_ge(rows_added, CHUNKS + 1)
            for b in range(BASES):
                second_product(1, b)
            pe.wait_ge(deg_part_ready, 1)
            for t, r in tiles:
                last = nc.tensor.matmul(bank[1][0:r, t:t + 1], deg_part[:, t * P:t * P + r], ones16[:, 0:1],
                                        start=True, stop=True)
            last.then_inc(deg_summed, 1)
            narrow = is_narrow(pe)
            pe.wait_ge(sums_ready, 1)
            with pe.If(narrow):
                first_end(True)
                for n in range(1, len(blocks)):
                    pe.wait_ge(cnt16_act, n)
                    pe.wait_ge(cnt16_dve, n)
                    if n >= 2:
                        pe.wait_ge(agg_done, n - 1)
                    for t in range(TILES):
                        last = pair_products(n, t)
                        if t == TILES // 2:
                            project(n - 1)
                    last.then_inc(agg_ready, 1)
                project(len(blocks) - 1)
            with pe.Else():
                general_tensor(pe, 0)
                pe.wait_ge(sums_ready, 2)
                first_end(False)
                general_tensor(pe, 1)
                for n in range(len(blocks)):
                    project(n)


def kernel(x, src, dst, edge_type_32, edge_weight1, L0_gnn_weight, L0_gnn_w_comp, L0_gnn_loop_weight,
           L0_gnn_h_bias, L1_gnn_W, L1_gnn_b):
    import numpy as np
    import concourse.bacc as bacc
    from concourse.bass_utils import run_bass_kernel_spmd

    def arr(a):
        return np.ascontiguousarray(a)

    pad = CHUNKS * P - EDGES
    src, dst, types = (np.asarray(a) for a in (src, dst, edge_type_32))
    src_p = np.pad(src, (0, pad)).reshape(CHUNKS, P)
    dst_p = np.pad(dst, (0, pad), constant_values=-1).reshape(CHUNKS, P)
    norm_p = np.pad(np.asarray(edge_weight1)[:, 0], (0, pad)).reshape(CHUNKS, P)
    step = STEP * P
    arrays = {
        "x": arr(x),
        "src_idx": arr(np.pad(src_p, ((0, STEP), (0, 0))).reshape(STEPS + 1, 2, GROUP, P).transpose(0, 1, 3, 2)),
        "src_t": arr(src_p.T), "dst_t": arr(dst_p.T), "src_rows": arr(src_p), "dst_rows": arr(dst_p),
        "starts": arr(np.pad(dst[::P], (LEAD, 0))[None]),
        "types": arr(np.pad(types, (0, pad + step)).reshape(STEPS + 1, Q, 1, Q * P)),
        "type_rows": arr(np.pad(types, (0, pad)).reshape(CHUNKS, P)),
        "norm_t": arr(norm_p.T),
        "weight": arr(L0_gnn_weight), "w_comp": arr(L0_gnn_w_comp), "loop_w": arr(L0_gnn_loop_weight),
        "bias0": arr(L0_gnn_h_bias), "w1": arr(L1_gnn_W), "bias1": arr(L1_gnn_b),
    }
    nc = bacc.Bacc("TRN2", target_bir_lowering=False, num_devices=1)
    args = [nc.dram_tensor(name, a.shape, mybir.dt.from_np(a.dtype), kind="ExternalInput").ap()
            for name, a in arrays.items()]
    out = nc.dram_tensor("out", (NODES, FEAT), F32, kind="ExternalOutput").ap()
    gnn_kernel(nc, *args, out)
    result = run_bass_kernel_spmd(nc, [arrays], core_ids=[0])
    return result.results[0]["out"]
```
